# Optimizing a Trainium2 kernel written in Bass

```python
import numpy as np
import jax
import jax.numpy as jnp

def _softmax(x, axis=-1):
    return jax.nn.softmax(x, axis=axis)

def _gelu(x):
    return jax.nn.gelu(x, approximate=True)

def _silu(x):
    return jax.nn.silu(x)

def _sigmoid(x):
    return jax.nn.sigmoid(x)

def _layernorm(x, axis=-1, eps=1e-05):
    m = jnp.mean(x, axis=axis, keepdims=True)
    v = jnp.var(x, axis=axis, keepdims=True)
    return (x - m) / jnp.sqrt(v + eps)

def _scatter_add(tgt, idx, src, axis=0):
    return tgt.at[idx].add(src)

def _segment_sum(src, seg, n):
    return jax.ops.segment_sum(src, seg, n)
kernel_name = 'mk_dlrm_tower_d1_rec_r8_ab31ef'

def setup_inputs(seed: int=0):
    np.random.seed(seed)
    _w = jnp.asarray

    def _rec_inputs():
        import jax
        import jax.numpy as jnp
        _tk = jax.random.key(seed)
        ids = jnp.stack([jax.random.randint(jax.random.fold_in(_tk, 200 + f), (512,), 0, v, jnp.int32) for f, v in enumerate([1000, 12500, 1250, 12500, 12500, 125000, 1000, 12500, 1000, 12500, 125000, 1250, 1250, 1250, 1250, 1000, 1250, 12500, 1000, 12500, 12500, 1000, 1000, 125000, 1000, 1250])], axis=1)
        tbl_0 = 0.05 * jax.random.normal(jax.random.fold_in(_tk, 500 + 0), (1000, 64), jnp.float32)
        tbl_1 = 0.05 * jax.random.normal(jax.random.fold_in(_tk, 500 + 1), (12500, 64), jnp.float32)
        tbl_2 = 0.05 * jax.random.normal(jax.random.fold_in(_tk, 500 + 2), (1250, 64), jnp.float32)
        tbl_3 = 0.05 * jax.random.normal(jax.random.fold_in(_tk, 500 + 3), (12500, 64), jnp.float32)
        tbl_4 = 0.05 * jax.random.normal(jax.random.fold_in(_tk, 500 + 4), (12500, 64), jnp.float32)
        tbl_5 = 0.05 * jax.random.normal(jax.random.fold_in(_tk, 500 + 5), (125000, 64), jnp.float32)
        tbl_6 = 0.05 * jax.random.normal(jax.random.fold_in(_tk, 500 + 6), (1000, 64), jnp.float32)
        tbl_7 = 0.05 * jax.random.normal(jax.random.fold_in(_tk, 500 + 7), (12500, 64), jnp.float32)
        tbl_8 = 0.05 * jax.random.normal(jax.random.fold_in(_tk, 500 + 8), (1000, 64), jnp.float32)
        tbl_9 = 0.05 * jax.random.normal(jax.random.fold_in(_tk, 500 + 9), (12500, 64), jnp.float32)
        tbl_10 = 0.05 * jax.random.normal(jax.random.fold_in(_tk, 500 + 10), (125000, 64), jnp.float32)
        tbl_11 = 0.05 * jax.random.normal(jax.random.fold_in(_tk, 500 + 11), (1250, 64), jnp.float32)
        tbl_12 = 0.05 * jax.random.normal(jax.random.fold_in(_tk, 500 + 12), (1250, 64), jnp.float32)
        tbl_13 = 0.05 * jax.random.normal(jax.random.fold_in(_tk, 500 + 13), (1250, 64), jnp.float32)
        tbl_14 = 0.05 * jax.random.normal(jax.random.fold_in(_tk, 500 + 14), (1250, 64), jnp.float32)
        tbl_15 = 0.05 * jax.random.normal(jax.random.fold_in(_tk, 500 + 15), (1000, 64), jnp.float32)
        tbl_16 = 0.05 * jax.random.normal(jax.random.fold_in(_tk, 500 + 16), (1250, 64), jnp.float32)
        tbl_17 = 0.05 * jax.random.normal(jax.random.fold_in(_tk, 500 + 17), (12500, 64), jnp.float32)
        tbl_18 = 0.05 * jax.random.normal(jax.random.fold_in(_tk, 500 + 18), (1000, 64), jnp.float32)
        tbl_19 = 0.05 * jax.random.normal(jax.random.fold_in(_tk, 500 + 19), (12500, 64), jnp.float32)
        tbl_20 = 0.05 * jax.random.normal(jax.random.fold_in(_tk, 500 + 20), (12500, 64), jnp.float32)
        tbl_21 = 0.05 * jax.random.normal(jax.random.fold_in(_tk, 500 + 21), (1000, 64), jnp.float32)
        tbl_22 = 0.05 * jax.random.normal(jax.random.fold_in(_tk, 500 + 22), (1000, 64), jnp.float32)
        tbl_23 = 0.05 * jax.random.normal(jax.random.fold_in(_tk, 500 + 23), (125000, 64), jnp.float32)
        tbl_24 = 0.05 * jax.random.normal(jax.random.fold_in(_tk, 500 + 24), (1000, 64), jnp.float32)
        tbl_25 = 0.05 * jax.random.normal(jax.random.fold_in(_tk, 500 + 25), (1250, 64), jnp.float32)
        _rk = jax.random.fold_in(_tk, 7)
        r_dense_t = 7.22013e-05 + 1.00017 * jax.random.normal(jax.random.fold_in(_rk, 101), (512, 256), jnp.float32)
        W_top1 = 0.0360844 * jax.random.normal(jax.random.fold_in(_tk, 801), (768, 512), jnp.float32)
        W_top2 = 0.0441942 * jax.random.normal(jax.random.fold_in(_tk, 802), (512, 256), jnp.float32)
        W_top3 = 0.0625 * jax.random.normal(jax.random.fold_in(_tk, 803), (256, 1), jnp.float32)
        b_top1 = jnp.zeros((512,), jnp.float32)
        b_top2 = jnp.zeros((256,), jnp.float32)
        return (r_dense_t, ids, tbl_0, tbl_1, tbl_2, tbl_3, tbl_4, tbl_5, tbl_6, tbl_7, tbl_8, tbl_9, tbl_10, tbl_11, tbl_12, tbl_13, tbl_14, tbl_15, tbl_16, tbl_17, tbl_18, tbl_19, tbl_20, tbl_21, tbl_22, tbl_23, tbl_24, tbl_25, W_top1, b_top1, W_top2, b_top2, W_top3)
    r_dense_t, ids, tbl_0, tbl_1, tbl_2, tbl_3, tbl_4, tbl_5, tbl_6, tbl_7, tbl_8, tbl_9, tbl_10, tbl_11, tbl_12, tbl_13, tbl_14, tbl_15, tbl_16, tbl_17, tbl_18, tbl_19, tbl_20, tbl_21, tbl_22, tbl_23, tbl_24, tbl_25, W_top1, b_top1, W_top2, b_top2, W_top3 = _rec_inputs()

    def _L0_rec_setup():
        import jax, jax.numpy as jnp
        import numpy as np
        EPS = 1e-05
        NI = 33
        TRIL_I, TRIL_J = np.tril_indices(NI, k=-1)

        def layer_norm(x, g, b):
            m = jnp.mean(x, axis=-1, keepdims=True)
            v = jnp.mean(jnp.square(x - m), axis=-1, keepdims=True)
            return (x - m) * jax.lax.rsqrt(v + EPS) * g + b
        key = jax.random.key(seed)
        ks = jax.random.split(key, 8)
        B, D_DENSE, N_SP, D_SP = (4096, 256, 26, 64)
        E, PROJ, MAXD, NFLAT = (128, 32, 512, 528)
        dense_t = jax.random.normal(ks[0], (B, D_DENSE), dtype=jnp.float32)
        sparse_t = jax.random.normal(ks[1], (B, N_SP, D_SP), dtype=jnp.float32)
        Wd = jax.random.normal(ks[2], (E, D_DENSE), dtype=jnp.float32) / np.sqrt(D_DENSE)
        Ws = jax.random.normal(ks[3], (E, D_SP), dtype=jnp.float32) / np.sqrt(D_SP)
        Wsi = jax.random.normal(ks[4], (PROJ, N_SP), dtype=jnp.float32) / np.sqrt(N_SP)
        Wl = jax.random.normal(ks[5], (MAXD, NFLAT), dtype=jnp.float32) / np.sqrt(NFLAT)
        gd = jnp.ones((E,), jnp.float32)
        bd = jnp.zeros((E,), jnp.float32)
        gs = jnp.ones((E,), jnp.float32)
        bs = jnp.zeros((E,), jnp.float32)
        gsi = jnp.ones((PROJ,), jnp.float32)
        bsi = jnp.zeros((PROJ,), jnp.float32)
        gl = jnp.ones((MAXD,), jnp.float32)
        bl = jnp.zeros((MAXD,), jnp.float32)
        return {'dense_t': dense_t, 'sparse_t': sparse_t, 'Wd': Wd, 'gd': gd, 'bd': bd, 'Ws': Ws, 'gs': gs, 'bs': bs, 'Wsi': Wsi, 'gsi': gsi, 'bsi': bsi, 'Wl': Wl, 'gl': gl, 'bl': bl, 'dims_in_use': 384}
    _L0_rec_all = _L0_rec_setup()
    _L0_rec_in = {k: v for k, v in _L0_rec_all.items() if k in ('Wd', 'gd', 'bd', 'Ws', 'gs', 'bs', 'Wsi', 'gsi', 'bsi', 'Wl', 'gl', 'bl')}
    del _L0_rec_all
    return {'r_dense_t': r_dense_t, 'ids': ids, 'tbl_0': tbl_0, 'tbl_1': tbl_1, 'tbl_2': tbl_2, 'tbl_3': tbl_3, 'tbl_4': tbl_4, 'tbl_5': tbl_5, 'tbl_6': tbl_6, 'tbl_7': tbl_7, 'tbl_8': tbl_8, 'tbl_9': tbl_9, 'tbl_10': tbl_10, 'tbl_11': tbl_11, 'tbl_12': tbl_12, 'tbl_13': tbl_13, 'tbl_14': tbl_14, 'tbl_15': tbl_15, 'tbl_16': tbl_16, 'tbl_17': tbl_17, 'tbl_18': tbl_18, 'tbl_19': tbl_19, 'tbl_20': tbl_20, 'tbl_21': tbl_21, 'tbl_22': tbl_22, 'tbl_23': tbl_23, 'tbl_24': tbl_24, 'tbl_25': tbl_25, 'W_top1': W_top1, 'b_top1': b_top1, 'W_top2': W_top2, 'b_top2': b_top2, 'W_top3': W_top3, 'L0_rec_Wd': _L0_rec_in['Wd'], 'L0_rec_gd': _L0_rec_in['gd'], 'L0_rec_bd': _L0_rec_in['bd'], 'L0_rec_Ws': _L0_rec_in['Ws'], 'L0_rec_gs': _L0_rec_in['gs'], 'L0_rec_bs': _L0_rec_in['bs'], 'L0_rec_Wsi': _L0_rec_in['Wsi'], 'L0_rec_gsi': _L0_rec_in['gsi'], 'L0_rec_bsi': _L0_rec_in['bsi'], 'L0_rec_Wl': _L0_rec_in['Wl'], 'L0_rec_gl': _L0_rec_in['gl'], 'L0_rec_bl': _L0_rec_in['bl']}

def reference(r_dense_t, ids, tbl_0, tbl_1, tbl_2, tbl_3, tbl_4, tbl_5, tbl_6, tbl_7, tbl_8, tbl_9, tbl_10, tbl_11, tbl_12, tbl_13, tbl_14, tbl_15, tbl_16, tbl_17, tbl_18, tbl_19, tbl_20, tbl_21, tbl_22, tbl_23, tbl_24, tbl_25, W_top1, b_top1, W_top2, b_top2, W_top3, L0_rec_Wd, L0_rec_gd, L0_rec_bd, L0_rec_Ws, L0_rec_gs, L0_rec_bs, L0_rec_Wsi, L0_rec_gsi, L0_rec_bsi, L0_rec_Wl, L0_rec_gl, L0_rec_bl):
    import jax
    import jax.numpy as jnp

    def _L0_rec_ref(dense_t, sparse_t, Wd, gd, bd, Ws, gs, bs, Wsi, gsi, bsi, Wl, gl, bl, dims_in_use):
        import jax, jax.numpy as jnp
        import numpy as np
        EPS = 1e-05
        NI = 33
        TRIL_I, TRIL_J = np.tril_indices(NI, k=-1)

        def layer_norm(x, g, b):
            m = jnp.mean(x, axis=-1, keepdims=True)
            v = jnp.mean(jnp.square(x - m), axis=-1, keepdims=True)
            return (x - m) * jax.lax.rsqrt(v + EPS) * g + b
        x = layer_norm(dense_t @ Wd.T, gd, bd)
        y = layer_norm(jnp.einsum('bnd,ed->bne', sparse_t, Ws), gs, bs)
        y = jnp.einsum('bne,pn->bep', y, Wsi)
        y = layer_norm(y, gsi, bsi)
        y = jnp.swapaxes(y, 1, 2)
        T = jnp.concatenate([x[:, None, :], y], axis=1)
        Z = jnp.einsum('bnd,bmd->bnm', T, T)
        Zflat = Z[:, TRIL_I, TRIL_J]
        out = layer_norm(Zflat @ Wl.T, gl, bl)
        maxd = out.shape[-1]
        mask = (jnp.arange(maxd) < dims_in_use).astype(out.dtype)
        return out * mask
    e = jnp.stack([tbl_0[ids[:, 0]], tbl_1[ids[:, 1]], tbl_2[ids[:, 2]], tbl_3[ids[:, 3]], tbl_4[ids[:, 4]], tbl_5[ids[:, 5]], tbl_6[ids[:, 6]], tbl_7[ids[:, 7]], tbl_8[ids[:, 8]], tbl_9[ids[:, 9]], tbl_10[ids[:, 10]], tbl_11[ids[:, 11]], tbl_12[ids[:, 12]], tbl_13[ids[:, 13]], tbl_14[ids[:, 14]], tbl_15[ids[:, 15]], tbl_16[ids[:, 16]], tbl_17[ids[:, 17]], tbl_18[ids[:, 18]], tbl_19[ids[:, 19]], tbl_20[ids[:, 20]], tbl_21[ids[:, 21]], tbl_22[ids[:, 22]], tbl_23[ids[:, 23]], tbl_24[ids[:, 24]], tbl_25[ids[:, 25]]], axis=1)
    z = _L0_rec_ref(r_dense_t, e, L0_rec_Wd, L0_rec_gd, L0_rec_bd, L0_rec_Ws, L0_rec_gs, L0_rec_bs, L0_rec_Wsi, L0_rec_gsi, L0_rec_bsi, L0_rec_Wl, L0_rec_gl, L0_rec_bl, 384)
    z = z.reshape(z.shape[0], -1)
    h = jnp.concatenate([z, r_dense_t], axis=1)
    h = jnp.maximum(h @ W_top1 + b_top1, 0.0)
    h = jnp.maximum(h @ W_top2 + b_top2, 0.0)
    y = h @ W_top3
    return y

_drawn_inputs = setup_inputs


def setup_inputs(seed=0):
    import zlib

    import numpy as np

    out = dict(_drawn_inputs(seed))
    spreads = {'b_top1': (0.0, 0.1),
     'b_top2': (0.0, 0.1),
     'L0_rec_gd': (1.0, 0.6),
     'L0_rec_bd': (0.0, 0.8),
     'L0_rec_gs': (1.0, 0.6),
     'L0_rec_bs': (0.0, 0.1),
     'L0_rec_gsi': (1.0, 0.2),
     'L0_rec_bsi': (0.0, 0.267),
     'L0_rec_gl': (1.0, 0.2),
     'L0_rec_bl': (0.0, 0.1)}
    factors = {}
    for name, (base, spread) in spreads.items():
        noise = np.random.default_rng([zlib.crc32(name.encode()), seed]).standard_normal(out[name].shape)
        drawn = base * np.exp(spread * noise) if base else spread * noise
        out[name] = jnp.asarray(drawn.astype(out[name].dtype))
    for name, factor in factors.items():
        out[name] = (out[name] * factor).astype(out[name].dtype)
    return out
```

```python
from contextlib import ExitStack

import numpy as np

import concourse.bass as bass
from concourse import mybir

ALU = mybir.AluOpType
ACT = mybir.ActivationFunctionType
AX = mybir.AxisListType
F32 = mybir.dt.float32
I32 = mybir.dt.int32

P = 128
BATCH = 512
TILES = BATCH // P
NT = 26
D = 64
E = 128
PROJ = 32
HALVES = 2
HALF = P // HALVES
GATHERS = HALF * NT // P
BLOCKS = 4
BS = HALF // BLOCKS
MB = HALVES * BS
COLS = BS * PROJ
SLOTS = PROJ + 2
ZC = PROJ + 1
DENSE = 256
DK = DENSE // P
MAXD = 512
DIMS = 384
ZK = DIMS // P
H1 = 512
H2 = 256
EPS = 1e-5
PAIR_CHUNKS = 5
FEATS = PAIR_CHUNKS + 1
AUX = P - PROJ
SX, ONE = AUX - 2, AUX - 1


def new_gathers(j):
    first = -(-j * BS * NT // P)
    return range(first, -(-(j + 1) * BS * NT // P))


def block_gathers(j):
    out = []
    for i in range(GATHERS):
        lo = max(i * P // NT, j * BS)
        hi = min(((i + 1) * P - 1) // NT, (j + 1) * BS - 1)
        if lo <= hi:
            out.append((i, lo - j * BS, hi - lo + 1))
    return out


SPREADS = [(j, i, lo, n) for j in range(BLOCKS) for i, lo, n in block_gathers(j)]
SPREAD_AT = np.concatenate([[0], np.cumsum([n for _, _, _, n in SPREADS])]).astype(int)


def pair_chunks():
    def rect(js, lo):
        return [(j, i) for j in js for i in range(lo[0], lo[1])]
    return [rect(range(0, 4), (0, 32)), rect(range(4, 8), (0, 32)), rect(range(8, 16), (8, 24)),
            rect(range(16, 24), (16, 32)), rect(list(range(8, 16)) + list(range(24, 32)), (24, 32))]


def columns(widths):
    at, out = 0, {}
    for name, w in widths:
        out[name] = (at, at + w)
        at += w
    return out, at


VEC, VECS = columns([("gs", 1), ("gd", 1), ("bd", 1), ("gl", ZK), ("bl", ZK), ("b1", H1 // P), ("b2", H2 // P),
                     ("w3", H2 // P), ("gi", 5), ("bi", 5), ("gj", 5), ("bj", 5)])
CON, CONS = columns([("ident", P), ("centre", P), ("pick_i", 5 * PROJ), ("pick_j", 5 * PROJ), ("is_x", 5),
                     ("not_x", 5), ("spread", int(SPREAD_AT[-1]))])


def build(nc, table, ids, offsets, dense, consts, vecs, bs_row, wd_t, ws2, wsi_rep, wl_t, w1_t, w2_t, out):
    with ExitStack() as ctx:
        def sb(name, shape, dt=F32):
            return ctx.enter_context(nc.sbuf_tensor(name, shape, dt))

        def sem(name):
            return ctx.enter_context(nc.semaphore(name))

        banks = [ctx.enter_context(nc.psum_tensor(f"bank{i}", [P, 512], F32)) for i in range(8)]
        turn_ps, gram_ps, spread_ps, proj_a_ps, proj_b_ps, pair_ps, wide_ps, misc_ps = banks

        con = sb("con", [P, CONS])
        vec = sb("vec", [P, VECS])
        ids_raw = sb("ids_raw", [TILES * HALVES * GATHERS, P], I32)
        ids_off = sb("ids_off", [TILES * HALVES * GATHERS, P])
        ids_sum = sb("ids_sum", [TILES * HALVES * GATHERS, P])
        idx = sb("idx", [P, TILES * HALVES * GATHERS], I32)
        bs_b = sb("bs_b", [NT, E])
        ws_sb = sb("ws_sb", [E, 2 * D])
        ws_c = sb("ws_c", [E, 2 * D])
        ws_cg = sb("ws_cg", [E, 2 * D])
        gram = sb("gram", [P, P])
        proj_w = sb("proj_w", [P, HALVES, E])
        wsi_raw = sb("wsi_raw", [P, GATHERS, PROJ])
        wsi_mean = sb("wsi_mean", [P, GATHERS])
        wsi_m = sb("wsi_m", [P, GATHERS])
        wsi_c = sb("wsi_c", [P, GATHERS, PROJ])
        spread = sb("spread", [P, int(SPREAD_AT[-1]), PROJ])
        shift = sb("shift", [E, PROJ])
        wd = sb("wd", [P, DK, E])
        dense_sb = sb("dense_sb", [P, TILES, DENSE])
        dense_t = sb("dense_t", [P, TILES, DK, P])
        wl = sb("wl", [P, FEATS, MAXD])
        w1 = sb("w1", [P, ZK + DK, H1])
        w2 = sb("w2", [P, H1 // P, H2])
        gj = sb("gj", [P, PAIR_CHUNKS])
        gj0 = sb("gj0", [P, PAIR_CHUNKS])
        bj = sb("bj", [P, PAIR_CHUNKS])
        gij = sb("gij", [P, PAIR_CHUNKS])
        aux_w = sb("aux_w", [P, PAIR_CHUNKS, P])
        aux_i = sb("aux_i", [P, PAIR_CHUNKS, PROJ])
        aux_j = sb("aux_j", [P, PAIR_CHUNKS, PROJ])
        ones = sb("ones", [P, 2])
        eps = sb("eps", [P, 1])
        x_stats = sb("x_stats", [P, 6])
        x_mv = sb("x_mv", [P, 2])
        x_rstd = sb("x_rstd", [P, 2])
        x_n = sb("x_n", [P, E])
        x_t = sb("x_t", [E, TILES, P])
        x_sum = sb("x_sum", [P, TILES])
        emb = sb("emb", [P, TILES, GATHERS, HALVES * D])
        emb_t = sb("emb_t", [P, 4 * P])
        prod = sb("prod", [P, 4 * P])
        var_e = sb("var_e", [P, 8])
        var_c = sb("var_c", [P, 8])
        std_e = sb("std_e", [P, 8])
        rstd_e = sb("rstd_e", [P, 8])
        emb_n = sb("emb_n", [P, 2, GATHERS, HALVES * D])
        spr = sb("spr", [P, COLS])
        y1 = sb("y1", [E, MB, PROJ])
        sq = sb("sq", [E, MB, PROJ])
        var_p = sb("var_p", [E, MB])
        std_p = sb("std_p", [E, MB])
        rstd_p = sb("rstd_p", [E, MB])
        terms = sb("terms", [E, 2, MB, SLOTS])
        pairs = sb("pairs", [P, ZC, PROJ])
        feats = sb("feats", [P, AUX + ZC * PROJ])
        packed = sb("packed", [P, 3, P])
        feats_t = sb("feats_t", [P, FEATS, P])
        z_stats = sb("z_stats", [P, 6])
        z_mv = sb("z_mv", [P, 2])
        z_rstd = sb("z_rstd", [P, 2])
        z_n = sb("z_n", [P, DIMS])
        z_t = sb("z_t", [P, ZK, P])
        h1_t = sb("h1_t", [P, H1 // P, P])
        h2_t = sb("h2_t", [P, H2 // P, P])
        y_row = sb("y_row", [1, BATCH])

        s_ids, s_con, s_vec, s_ws, s_wsi, s_bs, s_dense, s_wd, s_wl, s_w12, s_out = map(sem, (
            "s_ids", "s_con", "s_vec", "s_ws", "s_wsi", "s_bs", "s_dense", "s_wd", "s_wl", "s_w12", "s_out"))
        s_rows = [sem(f"s_rows{g}") for g in range(TILES * BLOCKS)]
        s_ids_sum, s_ids_t, s_idx = map(sem, ("s_ids_sum", "s_ids_t", "s_idx"))
        s_zeroed, s_ws_ps, s_ws_c, s_gram_ps, s_gram = map(sem, ("s_zeroed", "s_ws_ps", "s_ws_c", "s_gram_ps", "s_gram"))
        s_ws_cg, s_proj_ps, s_proj_w = map(sem, ("s_ws_cg", "s_proj_ps", "s_proj_w"))
        s_wsi_mean, s_wsi_m, s_wsi_c, s_spread, s_shift_ps, s_shift = map(sem, (
            "s_wsi_mean", "s_wsi_m", "s_wsi_c", "s_spread", "s_shift_ps", "s_shift"))
        s_pair_v, s_aux_ij, s_aux_w, s_wl_aux_ps, s_wl_aux, s_wl_g = map(sem, (
            "s_pair_v", "s_aux_ij", "s_aux_w", "s_wl_aux_ps", "s_wl_aux", "s_wl_g"))
        s_dt_ps, s_dt, s_x_ps, s_x_stats, s_x_mv, s_x_std, s_x_rstd, s_x_n, s_xt_ps, s_xt, s_xs_ps, s_xs = map(sem, (
            "s_dt_ps", "s_dt", "s_x_ps", "s_x_stats", "s_x_mv", "s_x_std", "s_x_rstd", "s_x_n", "s_xt_ps", "s_xt",
            "s_xs_ps", "s_xs"))
        s_turn, s_emb_t, s_gram_rows, s_prod, s_var_e, s_var_c, s_std_e, s_rstd_e, s_emb_n = map(sem, (
            "s_turn", "s_emb_t", "s_gram_rows", "s_prod", "s_var_e", "s_var_c", "s_std_e", "s_rstd_e", "s_emb_n"))
        s_spread_ps, s_spr, s_proj, s_y1, s_sq, s_var_p, s_std_p, s_rstd_p, s_terms, s_pair_ps, s_pairs = map(sem, (
            "s_spread_ps", "s_spr", "s_proj", "s_y1", "s_sq", "s_var_p", "s_std_p", "s_rstd_p", "s_terms",
            "s_pair_ps", "s_pairs"))
        s_packed = sem("s_packed")
        s_feats, s_ft_ps, s_ft, s_wide, s_z_stats, s_z_mv, s_z_std, s_z_rstd, s_z_n, s_zt_ps, s_zt = map(sem, (
            "s_feats", "s_ft_ps", "s_ft", "s_wide", "s_z_stats", "s_z_mv", "s_z_std", "s_z_rstd", "s_z_n", "s_zt_ps",
            "s_zt"))
        s_h1_ps, s_h1, s_h2_ps, s_h2, s_y_ps, s_y = map(sem, ("s_h1_ps", "s_h1", "s_h2_ps", "s_h2", "s_y_ps", "s_y"))

        def c(name):
            a, b = CON[name]
            return con[:, a:b]

        def v(name, k=0):
            a = VEC[name][0] + k
            return vec[:, a:a + 1]

        ident = c("ident")
        BLOCKS_ALL = TILES * BLOCKS

        block = ctx.enter_context(nc.Block())

        @block.sync
        def _(sp):
            sp.dma_start(ids_raw[:], ids).then_inc(s_ids, 16)
            sp.dma_start(ids_off[:], offsets).then_inc(s_ids, 16)
            sp.dma_start(con[:], consts).then_inc(s_con, 16)
            sp.dma_start(ws_sb[:], ws2).then_inc(s_ws, 16)
            sp.dma_start(wsi_raw[:], wsi_rep.rearrange("i p c -> p i c")).then_inc(s_wsi, 16)
            sp.dma_start(vec[:], vecs).then_inc(s_vec, 16)
            sp.dma_start(bs_b[:], bs_row.to_broadcast([NT, E])).then_inc(s_bs, 16)
            sp.dma_start(dense_sb[:], dense.rearrange("t p c -> p t c")).then_inc(s_dense, 16)
            sp.dma_start(wd[:], wd_t.rearrange("(k p) e -> p k e", p=P)).then_inc(s_wd, 16)
            sp.dma_start(wl[:, 0:PAIR_CHUNKS, :], wl_t.rearrange("(k p) o -> p k o", p=P)).then_inc(s_wl, 16)
            sp.dma_start(w1[:], w1_t.rearrange("(k p) o -> p k o", p=P)).then_inc(s_w12, 16)
            sp.dma_start(w2[:], w2_t.rearrange("(k p) o -> p k o", p=P)).then_inc(s_w12, 16)
            sp.wait_ge(s_y, TILES)
            sp.dma_start(out, y_row[:]).then_inc(s_out, 16)
            sp.wait_ge(s_out, 16)

        @block.gpsimd
        def _(pool):
            pool.memset(gram[:], 0.0).then_inc(s_zeroed, 1)
            pool.memset(proj_w[:], 0.0).then_inc(s_zeroed, 1)
            pool.memset(ones[:], 1.0).then_inc(s_zeroed, 1)
            pool.memset(eps[:], EPS).then_inc(s_zeroed, 1)
            pool.memset(terms[:, :, :, 0:1], 1.0).then_inc(s_zeroed, 1)
            pool.memset(feats[:, 0:SX], 0.0).then_inc(s_zeroed, 1)
            pool.memset(feats[:, ONE:ONE + 1], 1.0).then_inc(s_zeroed, 1)
            pool.memset(aux_w[:], 0.0).then_inc(s_zeroed, 1)
            pool.wait_ge(s_idx, 1)
            for t in range(TILES):
                for j in range(BLOCKS):
                    for i in new_gathers(j):
                        for h in range(HALVES):
                            at = (t * HALVES + h) * GATHERS + i
                            pool.indirect_dma_start(
                                emb[:, t, i, h * D:(h + 1) * D], None, table,
                                bass.IndirectOffsetOnAxis(ap=idx[:, at:at + 1], axis=0),
                            ).then_inc(s_rows[t * BLOCKS + j], 16)

        @block.tensor
        def _(pe):
            pe.wait_ge(s_con, 16)
            pe.wait_ge(s_ids_sum, 1)
            n = TILES * HALVES * GATHERS
            pe.transpose(turn_ps[:, 0:n], ids_sum[:], ident[0:n, 0:n]).then_inc(s_ids_t, 1)
            pe.wait_ge(s_ws, 16)
            pe.matmul(gram_ps[:, 0:P], c("centre"), ws_sb[:], start=True, stop=True).then_inc(s_ws_ps, 1)
            pe.wait_ge(s_ws_c, 1)
            pe.matmul(spread_ps[:, 0:P], ws_c[:], ws_c[:], start=True, stop=True).then_inc(s_gram_ps, 1)
            pe.wait_ge(s_ws_cg, 1)
            pe.transpose(proj_a_ps[:, 0:P], ws_cg[:], ident).then_inc(s_proj_ps, 1)
            pe.wait_ge(s_bs, 16)
            pe.wait_ge(s_wsi_c, 1)
            pe.matmul(proj_b_ps[:, 0:PROJ], bs_b[:], wsi_c[0:NT, 0, :], start=True, stop=True).then_inc(s_shift_ps, 1)
            pe.wait_ge(s_dense, 16)
            pe.wait_ge(s_wd, 16)
            for t in range(TILES):
                if t:
                    pe.wait_ge(s_dt, t)
                for k in range(DK):
                    last = pe.transpose(misc_ps[:, k * P:(k + 1) * P], dense_sb[:, t, k * P:(k + 1) * P], ident)
                last.then_inc(s_dt_ps, 1)
                pe.wait_ge(s_dt, t + 1)
                if t:
                    pe.wait_ge(s_x_n, t)
                for k in range(DK):
                    last = pe.matmul(wide_ps[:, 0:E], dense_t[:, t, k, :], wd[:, k, :],
                                     start=(k == 0), stop=(k == DK - 1))
                last.then_inc(s_x_ps, 1)
                pe.wait_ge(s_x_n, t + 1)
                if t:
                    pe.wait_ge(s_xt, t)
                pe.transpose(pair_ps[:, 0:P], x_n[:], ident).then_inc(s_xt_ps, 1)
                pe.wait_ge(s_xt, t + 1)
                if t:
                    pe.wait_ge(s_xs, t)
                pe.matmul(wide_ps[:, E:E + 1], x_t[:, t, :], ones[:, 0:1], start=True, stop=True).then_inc(s_xs_ps, 1)
            pe.wait_ge(s_wl, 16)
            pe.wait_ge(s_aux_w, 3)
            pe.wait_ge(s_xs, TILES)
            for k in range(PAIR_CHUNKS):
                last = pe.matmul(wide_ps[:], aux_w[:, k, :], wl[:, k, :], start=(k == 0), stop=(k == PAIR_CHUNKS - 1))
            last.then_inc(s_wl_aux_ps, 1)

            def turn(g):
                t, j = divmod(g, BLOCKS)
                pe.wait_ge(s_rows[g], 16 * HALVES * len(new_gathers(j)))
                if g == 0:
                    pe.wait_ge(s_idx, 1)
                if g:
                    pe.wait_ge(s_emb_t, g)
                for n, i in enumerate(new_gathers(j)):
                    last = pe.transpose(turn_ps[:, n * P:(n + 1) * P], emb[:, t, i, :], ident)
                last.then_inc(s_turn, 1)

            def gram_rows(g):
                pe.wait_ge(s_emb_t, g + 1)
                if g == 0:
                    pe.wait_ge(s_gram, 2)
                if g:
                    pe.wait_ge(s_prod, g)
                for n, _ in enumerate(new_gathers(g % BLOCKS)):
                    last = pe.matmul(gram_ps[:, n * P:(n + 1) * P], emb_t[:, n * P:(n + 1) * P], gram[:],
                                     start=True, stop=True)
                last.then_inc(s_gram_rows, 1)

            def spread_rows(g):
                t, j = divmod(g, BLOCKS)
                pe.wait_ge(s_emb_n, g + 1)
                if g == 0:
                    pe.wait_ge(s_spread, len(SPREADS))
                if g:
                    pe.wait_ge(s_spr, g)
                mine = [k for k, s in enumerate(SPREADS) if s[0] == j]
                for k in mine:
                    _, i, lo, n = SPREADS[k]
                    last = pe.matmul(spread_ps[:, lo * PROJ:(lo + n) * PROJ], emb_n[:, t % 2, i, :],
                                     spread[:, SPREAD_AT[k]:SPREAD_AT[k + 1], :], start=(k == mine[0]),
                                     stop=(k == mine[-1]), skip_group_check=True)
                last.then_inc(s_spread_ps, 1)

            def project(g):
                pe.wait_ge(s_spr, g + 1)
                if g == 0:
                    pe.wait_ge(s_proj_w, HALVES)
                    pe.wait_ge(s_shift, 1)
                if g:
                    pe.wait_ge(s_y1, HALVES * g)
                for h, bank in enumerate((proj_a_ps, proj_b_ps)):
                    pe.matmul(bank[:], proj_w[:, h, :], spr[:], start=True, stop=True).then_inc(s_proj, 1)

            def pair(g):
                pe.wait_ge(s_terms, g + 1)
                if g:
                    pe.wait_ge(s_pairs, g)
                for m in range(MB):
                    q, b = divmod(m, MB // 4)
                    last = pe.matmul(pair_ps[PROJ * q:PROJ * (q + 1), b * ZC:(b + 1) * ZC],
                                     terms[:, g % 2, m, 2:SLOTS], terms[:, g % 2, m, 0:ZC], start=True, stop=True,
                                     tile_position=(0, PROJ * q))
                last.then_inc(s_pair_ps, 1)

            def turn_feats(t, part):
                pe.wait_ge(s_feats, t + 1)
                if part == 0 and t:
                    pe.wait_ge(s_y, t)
                if part:
                    pe.wait_ge(s_ft, 2 * t + 1)
                if part == 0:
                    pe.wait_ge(s_packed, t + 1)
                parts = [feats[:, P:2 * P], feats[:, 2 * P:3 * P], packed[:, 0, :], packed[:, 1, :], packed[:, 2, :],
                         feats[:, 0:P]]
                for n, k in enumerate((range(0, 4), range(4, FEATS))[part]):
                    last = pe.transpose(misc_ps[:, n * P:(n + 1) * P], parts[k], ident)
                last.then_inc(s_ft_ps, 1)

            def wide(t):
                pe.wait_ge(s_ft, 2 * (t + 1))
                if t == 0:
                    pe.wait_ge(s_wl_g, PAIR_CHUNKS)
                    pe.wait_ge(s_wl_aux, 1)
                if t:
                    pe.wait_ge(s_h1, t)
                for k in range(FEATS):
                    last = pe.matmul(wide_ps[:], feats_t[:, k, :], wl[:, k, :], start=(k == 0), stop=(k == FEATS - 1))
                last.then_inc(s_wide, 1)

            def turn_z(t):
                pe.wait_ge(s_z_n, t + 1)
                for k in range(ZK):
                    last = pe.transpose(misc_ps[:, k * P:(k + 1) * P], z_n[:, k * P:(k + 1) * P], ident)
                last.then_inc(s_zt_ps, 1)

            def layer1(t):
                pe.wait_ge(s_zt, t + 1)
                if t == 0:
                    pe.wait_ge(s_w12, 32)
                for m in range(H1 // P):
                    for k in range(ZK + DK):
                        rhs = z_t[:, k, :] if k < ZK else dense_t[:, t, k - ZK, :]
                        last = pe.matmul(wide_ps[:, m * P:(m + 1) * P], w1[:, k, m * P:(m + 1) * P], rhs,
                                         start=(k == 0), stop=(k == ZK + DK - 1))
                last.then_inc(s_h1_ps, 1)

            def layer2(t):
                pe.wait_ge(s_h1, t + 1)
                for m in range(H2 // P):
                    for k in range(H1 // P):
                        last = pe.matmul(misc_ps[:, m * P:(m + 1) * P], w2[:, k, m * P:(m + 1) * P], h1_t[:, k, :],
                                         start=(k == 0), stop=(k == H1 // P - 1))
                last.then_inc(s_h2_ps, 1)

            def layer3(t):
                pe.wait_ge(s_h2, t + 1)
                for k in range(H2 // P):
                    last = pe.matmul(misc_ps[0:1, 2 * P:3 * P], v("w3", k), h2_t[:, k, :],
                                     start=(k == 0), stop=(k == H2 // P - 1))
                last.then_inc(s_y_ps, 1)

            for s in range(BLOCKS_ALL + 4):
                t, j = divmod(s - 6, BLOCKS)
                if s < BLOCKS_ALL:
                    turn(s)
                if t >= 0 and j == 0:
                    turn_feats(t, 0)
                if t >= 0 and j == 1:
                    turn_z(t)
                if 1 <= s <= BLOCKS_ALL:
                    spread_rows(s - 1)
                if t >= 0 and j == 0:
                    turn_feats(t, 1)
                if t >= 0 and j == 1:
                    layer1(t)
                if s < BLOCKS_ALL:
                    gram_rows(s)
                if t >= 0 and j == 1:
                    layer2(t)
                if 1 <= s <= BLOCKS_ALL:
                    project(s - 1)
                if t >= 0 and j == 0:
                    wide(t)
                if t >= 0 and j == 1:
                    layer3(t)
                if 2 <= s <= BLOCKS_ALL + 1:
                    pair(s - 2)

        @block.scalar
        def _(act):
            act.wait_ge(s_ws_ps, 1)
            act.copy(ws_c[:], gram_ps[:, 0:P]).then_inc(s_ws_c, 1)
            act.wait_ge(s_gram_ps, 1)
            act.wait_ge(s_zeroed, 8)
            for h in range(HALVES):
                a = slice(h * D, (h + 1) * D)
                act.mul(gram[a, a], spread_ps[a, a], 1.0 / E).then_inc(s_gram, 1)
            act.wait_ge(s_proj_ps, 1)
            for h in range(HALVES):
                a = slice(h * D, (h + 1) * D)
                act.copy(proj_w[a, h, :], proj_a_ps[a, 0:E]).then_inc(s_proj_w, 1)
            act.wait_ge(s_shift_ps, 1)
            act.copy(shift[:], proj_b_ps[:, 0:PROJ]).then_inc(s_shift, 1)
            act.wait_ge(s_vec, 16)
            for t in range(TILES):
                act.wait_ge(s_dt_ps, t + 1)
                act.copy(dense_t[:, t, :, :], misc_ps[:, 0:DK * P].rearrange("p (k b) -> p k b", b=P)).then_inc(s_dt, 1)
                act.wait_ge(s_x_mv, t + 1)
                act.activation(x_rstd[:, 0:1], x_mv[:, 1:2], ACT.Sqrt, bias=eps[:]).then_inc(s_x_std, 1)
                act.wait_ge(s_xt_ps, t + 1)
                act.activation(x_t[:, t, :], pair_ps[:, 0:P], ACT.Identity, bias=v("bd"), scale=v("gd")).then_inc(s_xt, 1)
                act.wait_ge(s_xs_ps, t + 1)
                act.copy(x_sum[:, t:t + 1], wide_ps[:, E:E + 1]).then_inc(s_xs, 1)
            act.wait_ge(s_wl_aux_ps, 1)
            act.copy(wl[:, PAIR_CHUNKS, :], wide_ps[:]).then_inc(s_wl_aux, 1)

            def copy_turned(g):
                act.wait_ge(s_turn, g + 1)
                if g:
                    act.wait_ge(s_gram_rows, g)
                n = len(new_gathers(g % BLOCKS)) * P
                act.copy(emb_t[:, 0:n], turn_ps[:, 0:n]).then_inc(s_emb_t, 1)

            def copy_spread(g):
                act.wait_ge(s_spread_ps, g + 1)
                if g:
                    act.wait_ge(s_proj, HALVES * g)
                act.copy(spr[:], spread_ps[:]).then_inc(s_spr, 1)

            def row_std(g):
                act.wait_ge(s_var_c, g + 1)
                if g:
                    act.wait_ge(s_rstd_e, g)
                n = HALVES * len(new_gathers(g % BLOCKS))
                act.activation(std_e[:, 0:n], var_c[:, 0:n], ACT.Sqrt, bias=eps[:]).then_inc(s_std_e, 1)

            def proj_std(g):
                act.wait_ge(s_var_p, g + 1)
                if g:
                    act.wait_ge(s_rstd_p, g)
                act.activation(std_p[:], var_p[:], ACT.Sqrt, bias=eps[:], scale=1.0 / PROJ).then_inc(s_std_p, 1)

            def z_std(t):
                act.wait_ge(s_z_mv, t + 1)
                act.activation(z_rstd[:, 0:1], z_mv[:, 1:2], ACT.Sqrt, bias=eps[:]).then_inc(s_z_std, 1)

            def squares(g):
                if g:
                    act.wait_ge(s_var_p, g)
                for h in range(HALVES):
                    a = slice(h * BS, (h + 1) * BS)
                    act.wait_ge(s_y1, HALVES * g + h + 1)
                    act.activation(sq[:, a, :], y1[:, a, :], ACT.Square).then_inc(s_sq, 1)

            def copy_pairs(g):
                t, j = divmod(g, BLOCKS)
                act.wait_ge(s_pair_ps, g + 1)
                if j == 0 and t:
                    act.wait_ge(s_feats, t)
                n = MB // 4
                act.copy(pairs[:, :, j * n:(j + 1) * n].rearrange("p j b -> p b j"),
                         pair_ps[:, 0:n * ZC].rearrange("p (b j) -> p b j", j=ZC)).then_inc(s_pairs, 1)

            def pack_pairs(t):
                act.wait_ge(s_feats, t + 1)
                if t:
                    act.wait_ge(s_ft_ps, 2 * t)
                grid = feats[:, P:AUX + ZC * PROJ].rearrange("b (j i) -> b j i", i=PROJ)
                act.copy(packed[:, 0, :].rearrange("b (j i) -> b j i", i=16), grid[:, 8:16, 8:24])
                act.copy(packed[:, 1, :].rearrange("b (j i) -> b j i", i=16), grid[:, 16:24, 16:32])
                act.copy(packed[:, 2, :].rearrange("b (a j i) -> b a j i", a=2, i=8),
                         grid[:, 8:, 24:32].rearrange("b (a j) i -> b a j i", j=8)[:, 0::2]).then_inc(s_packed, 1)

            def copy_feats(t, part):
                act.wait_ge(s_ft_ps, 2 * t + part + 1)
                if part == 0 and t:
                    act.wait_ge(s_wide, t)
                a, b = ((0, 4), (4, FEATS))[part]
                act.copy(feats_t[:, a:b, :], misc_ps[:, 0:(b - a) * P].rearrange("p (k b) -> p k b", b=P))\
                   .then_inc(s_ft, 1)

            def scale_z(t):
                act.wait_ge(s_zt_ps, t + 1)
                if t:
                    act.wait_ge(s_h1_ps, t)
                for k in range(ZK):
                    last = act.activation(z_t[:, k, :], misc_ps[:, k * P:(k + 1) * P], ACT.Identity,
                                          bias=v("bl", k), scale=v("gl", k))
                last.then_inc(s_zt, 1)

            def relu1(t):
                act.wait_ge(s_h1_ps, t + 1)
                if t:
                    act.wait_ge(s_h2_ps, t)
                for m in range(H1 // P):
                    last = act.activation(h1_t[:, m, :], wide_ps[:, m * P:(m + 1) * P], ACT.Relu, bias=v("b1", m))
                last.then_inc(s_h1, 1)

            def relu2(t):
                act.wait_ge(s_h2_ps, t + 1)
                if t:
                    act.wait_ge(s_y_ps, t)
                for m in range(H2 // P):
                    last = act.activation(h2_t[:, m, :], misc_ps[:, m * P:(m + 1) * P], ACT.Relu, bias=v("b2", m))
                last.then_inc(s_h2, 1)

            def copy_y(t):
                act.wait_ge(s_y_ps, t + 1)
                src = misc_ps[0:1, 2 * P:3 * P].rearrange("o (h q j b) -> o h j q b", h=2, q=2, j=BLOCKS)
                dst = y_row[0:1, t * P:(t + 1) * P].rearrange("o (h j q b) -> o h j q b", h=2, q=2, j=BLOCKS)
                for h in range(2):
                    last = act.copy(dst[:, h], src[:, h])
                last.then_inc(s_y, 1)

            for s in range(BLOCKS_ALL + 4):
                t, j = divmod(s - 6, BLOCKS)
                if t >= 0 and j == 0:
                    pack_pairs(t)
                if s < BLOCKS_ALL:
                    copy_turned(s)
                if t >= 0 and j == 0:
                    copy_feats(t, 0)
                if t >= 0 and j == 1:
                    scale_z(t)
                if 1 <= s <= BLOCKS_ALL:
                    copy_spread(s - 1)
                if t >= 0 and j == 0:
                    copy_feats(t, 1)
                if t >= 0 and j == 1:
                    relu1(t)
                    relu2(t)
                if s < BLOCKS_ALL:
                    row_std(s)
                if 1 <= s <= BLOCKS_ALL:
                    squares(s - 1)
                    proj_std(s - 1)
                if t >= 0 and j == 1:
                    copy_y(t)
                if t >= 0 and j == 0:
                    z_std(t)
                if 2 <= s <= BLOCKS_ALL + 1:
                    copy_pairs(s - 2)

        @block.vector
        def _(dve):
            dve.wait_ge(s_ids, 32)
            dve.tensor_tensor(ids_sum[:], ids_raw[:], ids_off[:], ALU.add).then_inc(s_ids_sum, 1)
            dve.wait_ge(s_ids_t, 1)
            dve.tensor_copy(idx[:], turn_ps[:, 0:TILES * HALVES * GATHERS]).then_inc(s_idx, 1)
            dve.wait_ge(s_vec, 16)
            dve.wait_ge(s_ws_c, 1)
            dve.tensor_scalar(ws_cg[:], ws_c[:], v("gs"), None, ALU.mult).then_inc(s_ws_cg, 1)
            dve.wait_ge(s_wsi, 16)
            dve.tensor_reduce(wsi_mean[:], wsi_raw[:], AX.X, ALU.add).then_inc(s_wsi_mean, 1)
            dve.wait_ge(s_wsi_mean, 1)
            dve.tensor_scalar(wsi_m[:], wsi_mean[:], 1.0 / PROJ, None, ALU.mult).then_inc(s_wsi_m, 1)
            dve.wait_ge(s_wsi_m, 1)
            dve.tensor_tensor(wsi_c[:], wsi_raw[:], wsi_m[:].unsqueeze(2).to_broadcast([P, GATHERS, PROJ]),
                              ALU.subtract).then_inc(s_wsi_c, 1)
            dve.wait_ge(s_con, 16)
            dve.wait_ge(s_wsi_c, 1)
            for k, (_, i, _, n) in enumerate(SPREADS):
                mask = c("spread")[:, SPREAD_AT[k]:SPREAD_AT[k + 1]]
                dve.tensor_tensor(spread[:, SPREAD_AT[k]:SPREAD_AT[k + 1], :],
                                  mask.unsqueeze(2).to_broadcast([P, n, PROJ]),
                                  wsi_c[:, i:i + 1, :].to_broadcast([P, n, PROJ]), ALU.mult).then_inc(s_spread, 1)

            for t in range(TILES):
                dve.wait_ge(s_x_ps, t + 1)
                dve.bn_stats(x_stats[:], wide_ps[:, 0:E]).then_inc(s_x_stats, 1)
                dve.wait_ge(s_x_stats, t + 1)
                dve.bn_aggr(x_mv[:], x_stats[:]).then_inc(s_x_mv, 1)
                dve.wait_ge(s_x_mv, t + 1)
                dve.wait_ge(s_x_std, t + 1)
                dve.reciprocal(x_rstd[:, 1:2], x_rstd[:, 0:1]).then_inc(s_x_rstd, 1)
                dve.wait_ge(s_x_rstd, t + 1)
                if t:
                    dve.wait_ge(s_xt_ps, t)
                dve.tensor_scalar(x_n[:], wide_ps[:, 0:E], x_mv[:, 0:1], x_rstd[:, 1:2], ALU.subtract, ALU.mult)\
                   .then_inc(s_x_n, 1)
            a, b = VEC["gj"]
            dve.tensor_tensor(gj0[:], vec[:, a:b], c("not_x"), ALU.mult).then_inc(s_pair_v, 1)
            a, b = VEC["bj"]
            dve.tensor_tensor(bj[:], vec[:, a:b], c("not_x"), ALU.mult).then_inc(s_pair_v, 1)
            dve.wait_ge(s_pair_v, 2)
            dve.tensor_tensor(gj[:], gj0[:], c("is_x"), ALU.add).then_inc(s_pair_v, 1)
            dve.wait_ge(s_pair_v, 3)
            a, b = VEC["gi"]
            dve.tensor_tensor(gij[:], vec[:, a:b], gj[:], ALU.mult).then_inc(s_pair_v, 1)
            dve.wait_ge(s_zeroed, 8)
            for k in range(PAIR_CHUNKS):
                pick_i = c("pick_i")[:, k * PROJ:(k + 1) * PROJ]
                pick_j = c("pick_j")[:, k * PROJ:(k + 1) * PROJ]
                dve.tensor_scalar(aux_i[:, k, :], pick_i, v("gi", k), bj[:, k:k + 1], ALU.mult, ALU.mult)
                dve.tensor_scalar(aux_j[:, k, :], pick_j, v("bi", k), gj[:, k:k + 1], ALU.mult, ALU.mult)\
                   .then_inc(s_aux_ij, 1)
            dve.wait_ge(s_aux_ij, PAIR_CHUNKS)
            a, b = VEC["bi"]
            dve.tensor_tensor(aux_w[:, :, AUX:P], aux_i[:], aux_j[:], ALU.add).then_inc(s_aux_w, 1)
            dve.tensor_tensor(aux_w[:, :, SX], vec[:, a:b], c("is_x"), ALU.mult).then_inc(s_aux_w, 1)
            dve.scalar_tensor_tensor(aux_w[:, :, ONE], vec[:, a:b], float(E), bj[:], ALU.mult, ALU.mult)\
               .then_inc(s_aux_w, 1)
            dve.wait_ge(s_pair_v, 4)
            dve.wait_ge(s_wl_aux_ps, 1)
            for k in range(PAIR_CHUNKS):
                dve.tensor_scalar(wl[:, k, :], wl[:, k, :], gij[:, k:k + 1], None, ALU.mult).then_inc(s_wl_g, 1)

            def row_variances(g):
                t, j = divmod(g, BLOCKS)
                rows = new_gathers(j)
                w = len(rows)
                e = emb[:, t, rows[0]:rows[0] + w, :]
                dve.wait_ge(s_gram_rows, g + 1)
                dve.tensor_tensor(prod[:, 0:w * P].rearrange("p (i c) -> p i c", c=P),
                                  gram_ps[:, 0:w * P].rearrange("p (i c) -> p i c", c=P), e, ALU.mult)\
                   .then_inc(s_prod, 1)
                dve.wait_ge(s_prod, g + 1)
                dve.tensor_reduce(var_e[:, 0:2 * w], prod[:, 0:w * P].rearrange("p (n d) -> p n d", d=D), AX.X,
                                  ALU.add).then_inc(s_var_e, 1)
                dve.wait_ge(s_var_e, g + 1)
                if g:
                    dve.wait_ge(s_std_e, g)
                dve.tensor_scalar(var_c[:, 0:2 * w], var_e[:, 0:2 * w], 0.0, None, ALU.max).then_inc(s_var_c, 1)

            def normalise_rows(g):
                t, j = divmod(g, BLOCKS)
                rows = new_gathers(j)
                w = len(rows)
                e = emb[:, t, rows[0]:rows[0] + w, :]
                dve.wait_ge(s_std_e, g + 1)
                dve.reciprocal(rstd_e[:, 0:2 * w], std_e[:, 0:2 * w]).then_inc(s_rstd_e, 1)
                dve.wait_ge(s_rstd_e, g + 1)
                if t >= 2:
                    dve.wait_ge(s_spread_ps, (t - 1) * BLOCKS)
                dve.tensor_tensor(emb_n[:, t % 2, rows[0]:rows[0] + w, :].rearrange("p i (h d) -> p (i h) d", d=D),
                                  e.rearrange("p i (h d) -> p (i h) d", d=D),
                                  rstd_e[:, 0:2 * w].unsqueeze(2).to_broadcast([P, 2 * w, D]), ALU.mult)\
                   .then_inc(s_emb_n, 1)

            def shift_rows(g):
                if g:
                    dve.wait_ge(s_terms, g)
                for h, bank in enumerate((proj_a_ps, proj_b_ps)):
                    dve.wait_ge(s_proj, HALVES * g + h + 1)
                    dve.tensor_tensor(y1[:, h * BS:(h + 1) * BS, :], bank[:].rearrange("e (b p) -> e b p", p=PROJ),
                                      shift[:].unsqueeze(1).to_broadcast([E, BS, PROJ]), ALU.add).then_inc(s_y1, 1)

            def normalise_proj(g):
                t, j = divmod(g, BLOCKS)
                dve.wait_ge(s_sq, HALVES * (g + 1))
                dve.tensor_reduce(var_p[:], sq[:], AX.X, ALU.add).then_inc(s_var_p, 1)
                if g >= 2:
                    dve.wait_ge(s_pair_ps, g - 1)
                x = x_t[:, t, :].rearrange("e (q j b) -> e q j b", q=4, j=BLOCKS)[:, :, j, :]
                dve.tensor_copy(terms[:, g % 2, :, 1].rearrange("e (q b) -> e q b", q=4), x)
                dve.wait_ge(s_std_p, g + 1)
                dve.reciprocal(rstd_p[:], std_p[:]).then_inc(s_rstd_p, 1)
                dve.wait_ge(s_rstd_p, g + 1)
                dve.tensor_tensor(terms[:, g % 2, :, 2:SLOTS], y1[:],
                                  rstd_p[:].unsqueeze(2).to_broadcast([E, MB, PROJ]), ALU.mult).then_inc(s_terms, 1)

            def turn_pairs(t):
                dve.wait_ge(s_pairs, BLOCKS * (t + 1))
                if t:
                    dve.wait_ge(s_ft_ps, 2 * t)
                dve.tensor_copy(feats[:, SX:SX + 1], x_sum[:, t:t + 1])
                dve.transpose(feats[:, AUX:AUX + ZC * PROJ], pairs[:].rearrange("p j b -> p (j b)")).then_inc(s_feats, 1)

            def normalise_z(t):
                dve.wait_ge(s_wide, t + 1)
                dve.bn_stats(z_stats[:], wide_ps[:]).then_inc(s_z_stats, 1)
                dve.wait_ge(s_z_stats, t + 1)
                dve.bn_aggr(z_mv[:], z_stats[:]).then_inc(s_z_mv, 1)
                dve.wait_ge(s_z_mv, t + 1)
                dve.wait_ge(s_z_std, t + 1)
                dve.reciprocal(z_rstd[:, 1:2], z_rstd[:, 0:1]).then_inc(s_z_rstd, 1)
                dve.wait_ge(s_z_rstd, t + 1)
                if t:
                    dve.wait_ge(s_zt_ps, t)
                dve.tensor_scalar(z_n[:], wide_ps[:, 0:DIMS], z_mv[:, 0:1], z_rstd[:, 1:2], ALU.subtract, ALU.mult)\
                   .then_inc(s_z_n, 1)

            for s in range(BLOCKS_ALL + 4):
                t, j = divmod(s - 6, BLOCKS)
                if t >= 0 and j == 0:
                    turn_pairs(t)
                if s < BLOCKS_ALL:
                    row_variances(s)
                if 1 <= s <= BLOCKS_ALL:
                    shift_rows(s - 1)
                if s < BLOCKS_ALL:
                    normalise_rows(s)
                if 1 <= s <= BLOCKS_ALL:
                    normalise_proj(s - 1)
                if t >= 0 and j == 0:
                    normalise_z(t)


def layout(inputs):
    tables = [np.asarray(inputs[f"tbl_{k}"]) for k in range(NT)]
    get = {k: np.asarray(a) for k, a in inputs.items() if not k.startswith("tbl_")}
    a = {"table": np.concatenate(tables, axis=0)}
    first = np.concatenate([[0], np.cumsum([x.shape[0] for x in tables])])[:NT]
    n = TILES * HALVES * GATHERS
    a["ids"] = get["ids"].reshape(n, P)
    a["offsets"] = np.tile(first, BATCH).reshape(n, P).astype(np.float32)
    a["dense"] = get["r_dense_t"].reshape(TILES, 2, BLOCKS, 2, 8, DENSE).transpose(0, 1, 3, 2, 4, 5)\
        .reshape(TILES, P, DENSE)
    a["wd_t"] = get["L0_rec_Wd"].T
    a["ws2"] = np.concatenate([get["L0_rec_Ws"]] * 2, axis=1)
    a["wsi_rep"] = np.tile(get["L0_rec_Wsi"].T, (HALF, 1)).reshape(GATHERS, P, PROJ)
    a["bs_row"] = get["L0_rec_bs"].reshape(1, E)
    chunks = pair_chunks()
    wl_t = get["L0_rec_Wl"].T
    packed = np.zeros((PAIR_CHUNKS, P, MAXD), np.float32)
    con = np.zeros((P, CONS), np.float32)
    vec = np.zeros((P, VECS), np.float32)

    def cols(name, k=0, w=1):
        return slice(CON[name][0] + k * w, CON[name][0] + (k + 1) * w)

    for k, chunk in enumerate(chunks):
        i = np.array([x[1] for x in chunk])
        j = np.array([x[0] for x in chunk])
        live = i >= j
        packed[k, live] = wl_t[(i * (i + 1) // 2 + j)[live]]
        con[np.arange(P), CON["pick_i"][0] + k * PROJ + i] = 1.0
        y = j >= 1
        con[np.arange(P)[y], CON["pick_j"][0] + k * PROJ + j[y] - 1] = 1.0
        con[:, CON["is_x"][0] + k] = ~y
        con[:, CON["not_x"][0] + k] = y
        for name, src, at in (("gi", "gsi", i), ("bi", "bsi", i), ("gj", "gsi", np.maximum(j - 1, 0)),
                              ("bj", "bsi", np.maximum(j - 1, 0))):
            vec[:, VEC[name][0] + k] = get[f"L0_rec_{src}"][at]
    a["wl_t"] = packed.reshape(PAIR_CHUNKS * P, MAXD)
    con[:, CON["ident"][0]:CON["ident"][1]] = np.eye(P)
    con[:, CON["centre"][0]:CON["centre"][1]] = np.eye(P) - 1.0 / P
    for k, (j, i, lo, m) in enumerate(SPREADS):
        sample = (i * P + np.arange(P)) // NT - j * BS - lo
        ok = (sample >= 0) & (sample < m)
        con[np.arange(P)[ok], CON["spread"][0] + SPREAD_AT[k] + sample[ok]] = 1.0
    for name, src, w in (("gs", "L0_rec_gs", 1), ("gd", "L0_rec_gd", 1), ("bd", "L0_rec_bd", 1),
                         ("gl", "L0_rec_gl", ZK), ("bl", "L0_rec_bl", ZK), ("b1", "b_top1", H1 // P),
                         ("b2", "b_top2", H2 // P), ("w3", "W_top3", H2 // P)):
        vec[:, VEC[name][0]:VEC[name][1]] = get[src].reshape(-1, P)[:w].T
    a["consts"], a["vecs"] = con, vec
    w_top1 = get["W_top1"]
    a["w1_t"] = np.concatenate([w_top1[0:DIMS], w_top1[MAXD:]], axis=0)
    a["w2_t"] = get["W_top2"]
    return a


_INS = ["table", "ids", "offsets", "dense", "consts", "vecs", "bs_row", "wd_t", "ws2", "wsi_rep", "wl_t", "w1_t", "w2_t"]


def kernel(**inputs):
    import concourse.bacc as bacc
    from concourse.bass_utils import run_bass_kernel_spmd

    nc = bacc.Bacc("TRN2", target_bir_lowering=False, num_devices=1)
    arrays, args = {}, []
    for name, a in layout(inputs).items():
        arrays[f"in_{name}"] = np.ascontiguousarray(a)
    for name in _INS:
        a = arrays[f"in_{name}"]
        args.append(nc.dram_tensor(f"in_{name}", a.shape, mybir.dt.from_np(a.dtype), kind="ExternalInput").ap())
    out = nc.dram_tensor("out_y", (1, BATCH), F32, kind="ExternalOutput").ap()
    build(nc, *args, out)
    r = run_bass_kernel_spmd(nc, [arrays], core_ids=[0])
    return r.results[0]["out_y"].reshape(BATCH, 1)
```

```python
from contextlib import ExitStack

import numpy as np

import concourse.bass as bass
from concourse import mybir

ALU = mybir.AluOpType
ACT = mybir.ActivationFunctionType
AX = mybir.AxisListType
F32 = mybir.dt.float32
I32 = mybir.dt.int32

P = 128
BATCH = 512
TILES = BATCH // P
NT = 26
D = 64
E = 128
PROJ = 32
HALVES = 2
HALF = P // HALVES
GATHERS = HALF * NT // P
BLOCKS = 4
BS = HALF // BLOCKS
MB = HALVES * BS
COLS = BS * PROJ
SLOTS = PROJ + 2
ZC = PROJ + 1
DENSE = 256
DK = DENSE // P
MAXD = 512
DIMS = 384
ZK = DIMS // P
H1 = 512
H2 = 256
EPS = 1e-5
PAIR_CHUNKS = 5
FEATS = PAIR_CHUNKS + 1
AUX = P - PROJ
SX, ONE = AUX - 2, AUX - 1


def new_gathers(j):
    first = -(-j * BS * NT // P)
    return range(first, -(-(j + 1) * BS * NT // P))


def block_gathers(j):
    out = []
    for i in range(GATHERS):
        lo = max(i * P // NT, j * BS)
        hi = min(((i + 1) * P - 1) // NT, (j + 1) * BS - 1)
        if lo <= hi:
            out.append((i, lo - j * BS, hi - lo + 1))
    return out


SPREADS = [(j, i, lo, n) for j in range(BLOCKS) for i, lo, n in block_gathers(j)]
SPREAD_AT = np.concatenate([[0], np.cumsum([n for _, _, _, n in SPREADS])]).astype(int)


def pair_chunks():
    def rect(js, lo):
        return [(j, i) for j in js for i in range(lo[0], lo[1])]
    return [rect(range(0, 4), (0, 32)), rect(range(4, 8), (0, 32)), rect(range(8, 16), (8, 24)),
            rect(range(16, 24), (16, 32)), rect(list(range(8, 16)) + list(range(24, 32)), (24, 32))]


def columns(widths):
    at, out = 0, {}
    for name, w in widths:
        out[name] = (at, at + w)
        at += w
    return out, at


VEC, VECS = columns([("gs", 1), ("gd", 1), ("bd", 1), ("gl", ZK), ("bl", ZK), ("b1", H1 // P), ("b2", H2 // P),
                     ("w3", H2 // P), ("gi", 5), ("bi", 5), ("gj", 5), ("bj", 5)])
CON, CONS = columns([("ident", P), ("centre", P), ("pick_i", 5 * PROJ), ("pick_j", 5 * PROJ), ("is_x", 5),
                     ("not_x", 5), ("spread", int(SPREAD_AT[-1]))])


def build(nc, table, ids, offsets, dense, consts, vecs, bs_row, wd_t, ws2, wsi_rep, wl_t, w1_t, w2_t, out):
    with ExitStack() as ctx:
        def sb(name, shape, dt=F32):
            return ctx.enter_context(nc.sbuf_tensor(name, shape, dt))

        def sem(name):
            return ctx.enter_context(nc.semaphore(name))

        banks = [ctx.enter_context(nc.psum_tensor(f"bank{i}", [P, 512], F32)) for i in range(8)]
        turn_ps, gram_ps, spread_ps, wide_ps, pair_ps = banks[0:3] + banks[6:8]
        proj_ps = banks[3:6]

        con = sb("con", [P, CONS])
        vec = sb("vec", [P, VECS])
        ids_raw = sb("ids_raw", [TILES * HALVES * GATHERS, P], I32)
        ids_off = sb("ids_off", [TILES * HALVES * GATHERS, P])
        ids_sum = sb("ids_sum", [TILES * HALVES * GATHERS, P])
        idx = sb("idx", [P, TILES * HALVES * GATHERS], I32)
        ws_sb = sb("ws_sb", [E, 2 * D])
        ws_c = sb("ws_c", [E, 2 * D])
        ws_cg = sb("ws_cg", [E, 2 * D])
        gram = sb("gram", [P, P])
        proj_w = sb("proj_w", [P, HALVES, E])
        wsi_raw = sb("wsi_raw", [P, GATHERS, PROJ])
        wsi_mean = sb("wsi_mean", [P, GATHERS])
        wsi_m = sb("wsi_m", [P, GATHERS])
        wsi_c = sb("wsi_c", [P, GATHERS, PROJ])
        spread = sb("spread", [P, int(SPREAD_AT[-1]), PROJ])
        wd = sb("wd", [P, DK, E])
        dense_sb = sb("dense_sb", [P, TILES, DENSE])
        dense_t = sb("dense_t", [P, TILES, DK, P])
        wl = sb("wl", [P, FEATS, MAXD])
        w1 = sb("w1", [P, ZK + DK, H1])
        w2 = sb("w2", [P, H1 // P, H2])
        gj = sb("gj", [P, PAIR_CHUNKS])
        gj0 = sb("gj0", [P, PAIR_CHUNKS])
        bj = sb("bj", [P, PAIR_CHUNKS])
        gij = sb("gij", [P, PAIR_CHUNKS])
        aux_w = sb("aux_w", [P, PAIR_CHUNKS, P])
        aux_i = sb("aux_i", [P, PAIR_CHUNKS, PROJ])
        aux_j = sb("aux_j", [P, PAIR_CHUNKS, PROJ])
        ones = sb("ones", [P, P])
        eps = sb("eps", [P, 1])
        x_stats = sb("x_stats", [P, TILES, 6])
        x_mv = sb("x_mv", [P, TILES, 2])
        x_std = sb("x_std", [P, TILES])
        x_rstd = sb("x_rstd", [P, TILES])
        x_n = sb("x_n", [P, TILES, E])
        x_t = sb("x_t", [E, TILES, P])
        x_sum = sb("x_sum", [P, TILES])
        emb = sb("emb", [P, TILES, GATHERS, HALVES * D])
        emb_t = sb("emb_t", [P, 2, 4 * P])
        prod = sb("prod", [P, 4 * P])
        var_e = sb("var_e", [P, 8])
        var_c = sb("var_c", [P, 8])
        std_e = sb("std_e", [P, 8])
        rstd_e = sb("rstd_e", [P, 8])
        emb_n = sb("emb_n", [P, 2, GATHERS, HALVES * D])
        spr = sb("spr", [P, 2, HALVES, COLS])
        sq = sb("sq", [E, MB, PROJ])
        var_p = sb("var_p", [E, MB])
        std_p = sb("std_p", [E, MB])
        rstd_p = sb("rstd_p", [E, MB])
        terms = sb("terms", [E, 2, MB, SLOTS])
        pairs = sb("pairs", [P, ZC, PROJ])
        feats = sb("feats", [P, AUX + ZC * PROJ])
        packed = sb("packed", [P, 3, P])
        feats_t = sb("feats_t", [P, FEATS, P])
        z_stats = sb("z_stats", [P, 6])
        z_mv = sb("z_mv", [P, 2])
        z_std_sb = sb("z_std_sb", [P, 1])
        z_rstd = sb("z_rstd", [P, 1])
        z_n = sb("z_n", [P, DIMS])
        z_t = sb("z_t", [P, ZK, P])
        h1_dense = sb("h1_dense", [P, H1 // P, BATCH])
        h1_sum = sb("h1_sum", [P, H1 // P, P])
        h1_t = sb("h1_t", [P, H1 // P, P])
        h2_t = sb("h2_t", [P, H2 // P, P])
        y_row = sb("y_row", [1, BATCH])

        s_ids, s_con, s_vec, s_ws, s_wsi, s_bs, s_dense, s_wd, s_wl, s_w12, s_out = map(sem, (
            "s_ids", "s_con", "s_vec", "s_ws", "s_wsi", "s_bs", "s_dense", "s_wd", "s_wl", "s_w12", "s_out"))
        s_rows = [sem(f"s_rows{g}") for g in range(TILES * BLOCKS)]
        s_ids_sum, s_ids_t, s_idx = map(sem, ("s_ids_sum", "s_ids_t", "s_idx"))
        s_zeroed_w, s_w1d, s_hd_ps, s_hd, s_h1_sum = map(sem, ("s_zeroed_w", "s_w1d", "s_hd_ps", "s_hd", "s_h1_sum"))
        s_zeroed, s_ws_ps, s_ws_c, s_gram_ps, s_gram = map(sem, ("s_zeroed", "s_ws_ps", "s_ws_c", "s_gram_ps", "s_gram"))
        s_ws_cg, s_proj_ps, s_proj_w = map(sem, ("s_ws_cg", "s_proj_ps", "s_proj_w"))
        s_wsi_mean, s_wsi_m, s_wsi_c, s_spread, s_shift_ps, s_shift = map(sem, (
            "s_wsi_mean", "s_wsi_m", "s_wsi_c", "s_spread", "s_shift_ps", "s_shift"))
        s_pair_v, s_aux_ij, s_aux_w, s_wl_aux_ps, s_wl_aux, s_wl_g = map(sem, (
            "s_pair_v", "s_aux_ij", "s_aux_w", "s_wl_aux_ps", "s_wl_aux", "s_wl_g"))
        s_dt_ps, s_dt, s_x_ps, s_x_stats, s_x_mv, s_x_std, s_x_rstd, s_x_n, s_xt_ps, s_xt, s_xs_ps, s_xs = map(sem, (
            "s_dt_ps", "s_dt", "s_x_ps", "s_x_stats", "s_x_mv", "s_x_std", "s_x_rstd", "s_x_n", "s_xt_ps", "s_xt",
            "s_xs_ps", "s_xs"))
        s_turn, s_emb_t, s_gram_rows, s_prod, s_var_e, s_var_c, s_std_e, s_rstd_e, s_emb_n = map(sem, (
            "s_turn", "s_emb_t", "s_gram_rows", "s_prod", "s_var_e", "s_var_c", "s_std_e", "s_rstd_e", "s_emb_n"))
        s_spread_ps, s_spr, s_proj, s_sq, s_var_p, s_std_p, s_rstd_p, s_terms, s_pair_ps, s_pairs = map(sem, (
            "s_spread_ps", "s_spr", "s_proj", "s_sq", "s_var_p", "s_std_p", "s_rstd_p", "s_terms",
            "s_pair_ps", "s_pairs"))
        s_packed = sem("s_packed")
        s_feats, s_ft_ps, s_ft, s_wide, s_z_stats, s_z_mv, s_z_std, s_z_rstd, s_z_n, s_zt_ps, s_z_t = map(sem, (
            "s_feats", "s_ft_ps", "s_ft", "s_wide", "s_z_stats", "s_z_mv", "s_z_std", "s_z_rstd", "s_z_n", "s_zt_ps",
            "s_z_t"))
        s_h1_ps, s_h1, s_h2_ps, s_h2, s_y_ps, s_y = map(sem, ("s_h1_ps", "s_h1", "s_h2_ps", "s_h2", "s_y_ps", "s_y"))

        def c(name):
            a, b = CON[name]
            return con[:, a:b]

        def v(name, k=0):
            a = VEC[name][0] + k
            return vec[:, a:a + 1]

        ident = c("ident")
        BLOCKS_ALL = TILES * BLOCKS
        FINISH = BLOCKS - 1 + 4
        LAST = BLOCKS * (TILES - 1) + FINISH + 4

        block = ctx.enter_context(nc.Block())

        @block.sync
        def _(sp):
            sp.dma_start(ids_raw[:], ids).then_inc(s_ids, 16)
            sp.dma_start(ids_off[:], offsets).then_inc(s_ids, 16)
            sp.dma_start(con[:], consts).then_inc(s_con, 16)
            sp.dma_start(ws_sb[:], ws2).then_inc(s_ws, 16)
            sp.dma_start(wsi_raw[:], wsi_rep.rearrange("i p c -> p i c")).then_inc(s_wsi, 16)
            sp.dma_start(vec[:], vecs).then_inc(s_vec, 16)
            sp.dma_start(dense_sb[:], dense.rearrange("t p c -> p t c")).then_inc(s_dense, 16)
            sp.dma_start(wd[:], wd_t.rearrange("(k p) e -> p k e", p=P)).then_inc(s_wd, 16)
            sp.dma_start(w1[:, ZK:ZK + DK, :], w1_t[DIMS:, :].rearrange("(k p) o -> p k o", p=P)).then_inc(s_w1d, 16)
            sp.wait_ge(s_zeroed_w, 4)
            sp.dma_start(proj_w[D:D + 1, 0, :], bs_row).then_inc(s_bs, 16)
            sp.dma_start(proj_w[0:1, 1, :], bs_row).then_inc(s_bs, 16)
            sp.dma_start(wl[:, 0:PAIR_CHUNKS, :], wl_t.rearrange("(k p) o -> p k o", p=P)).then_inc(s_wl, 16)
            sp.dma_start(w1[:, 0:ZK, :], w1_t[0:DIMS, :].rearrange("(k p) o -> p k o", p=P)).then_inc(s_w12, 16)
            sp.dma_start(w2[:], w2_t.rearrange("(k p) o -> p k o", p=P)).then_inc(s_w12, 16)
            sp.wait_ge(s_y, TILES)
            sp.dma_start(out, y_row[:]).then_inc(s_out, 16)
            sp.wait_ge(s_out, 16)

        @block.gpsimd
        def _(pool):
            pool.memset(ones[:], 1.0).then_inc(s_zeroed, 1)
            pool.memset(eps[:], EPS).then_inc(s_zeroed, 1)
            pool.memset(terms[:, :, :, 0:1], 1.0).then_inc(s_zeroed, 1)
            pool.memset(feats[:, 0:SX], 0.0).then_inc(s_zeroed, 1)
            pool.memset(feats[:, ONE:ONE + 1], 1.0).then_inc(s_zeroed, 1)
            pool.memset(aux_w[:], 0.0).then_inc(s_zeroed, 1)
            pool.wait_ge(s_idx, 1)
            for t in range(TILES):
                for j in range(BLOCKS):
                    for i in new_gathers(j):
                        for h in range(HALVES):
                            at = (t * HALVES + h) * GATHERS + i
                            pool.indirect_dma_start(
                                emb[:, t, i, h * D:(h + 1) * D], None, table,
                                bass.IndirectOffsetOnAxis(ap=idx[:, at:at + 1], axis=0),
                            ).then_inc(s_rows[t * BLOCKS + j], 16)

        @block.tensor
        def _(pe):
            pe.wait_ge(s_con, 16)
            pe.wait_ge(s_ids_sum, 1)
            n = TILES * HALVES * GATHERS
            pe.transpose(turn_ps[:, 0:n], ids_sum[:], ident[0:n, 0:n]).then_inc(s_ids_t, 1)
            pe.wait_ge(s_ws, 16)
            pe.matmul(gram_ps[:, 0:P], c("centre"), ws_sb[:], start=True, stop=True).then_inc(s_ws_ps, 1)
            pe.wait_ge(s_ws_c, 1)
            pe.matmul(spread_ps[:, 0:P], ws_c[:], ws_c[:], start=True, stop=True).then_inc(s_gram_ps, 1)
            pe.wait_ge(s_ws_cg, 1)
            pe.transpose(proj_ps[0][:, 0:P], ws_cg[:], ident).then_inc(s_proj_ps, 1)
            pe.wait_ge(s_zeroed, 6)
            pe.wait_ge(s_wsi_c, 1)
            pe.matmul(pair_ps[:, 0:PROJ], ones[0:NT, :], wsi_c[0:NT, 0, :], start=True, stop=True)\
              .then_inc(s_shift_ps, 1)
            pe.wait_ge(s_dense, 16)
            pe.wait_ge(s_proj_w, HALVES)
            for t in range(TILES):
                bank, at = proj_ps[1 + t // 2], (t % 2) * DK * P
                for k in range(DK):
                    last = pe.transpose(bank[:, at + k * P:at + (k + 1) * P], dense_sb[:, t, k * P:(k + 1) * P], ident)
                if t % 2:
                    last.then_inc(s_dt_ps, 1)
            pe.wait_ge(s_wd, 16)
            for t in range(TILES):
                if t % 2 == 0:
                    pe.wait_ge(s_dt, t // 2 + 1)
                for k in range(DK):
                    last = pe.matmul(proj_ps[0][:, t * P:(t + 1) * P], dense_t[:, t, k, :], wd[:, k, :],
                                     start=(k == 0), stop=(k == DK - 1))
            last.then_inc(s_x_ps, 1)

            def dense_layer1(m):
                pe.wait_ge(s_w1d, 16)
                if m >= 2:
                    pe.wait_ge(s_hd, m - 1)
                for k in range(DK):
                    last = pe.matmul(proj_ps[1 + m % 2][:], w1[:, ZK + k, m * P:(m + 1) * P], dense_t[:, :, k, :],
                                     start=(k == 0), stop=(k == DK - 1))
                last.then_inc(s_hd_ps, 1)

            dense_layer1(0)
            dense_layer1(1)
            for t in range(TILES):
                pe.wait_ge(s_x_n, t + 1)
                last = pe.transpose(wide_ps[:, t * P:(t + 1) * P], x_n[:, t, :], ident)
            last.then_inc(s_xt_ps, 1)

            def sum_x():
                pe.wait_ge(s_xt, 1)
                pe.wait_ge(s_shift, 1)
                for t in range(TILES):
                    last = pe.matmul(pair_ps[:, t:t + 1], x_t[:, t, :], ones[:, 0:1], start=True, stop=True)
                last.then_inc(s_xs_ps, 1)

            def aux_weights():
                pe.wait_ge(s_wl, 16)
                pe.wait_ge(s_aux_w, 3)
                for k in range(PAIR_CHUNKS):
                    last = pe.matmul(wide_ps[:], aux_w[:, k, :], wl[:, k, :], start=(k == 0),
                                     stop=(k == PAIR_CHUNKS - 1))
                last.then_inc(s_wl_aux_ps, 1)

            def turn_free(g):
                pe.wait_ge(s_emb_t, g)
                t, j = divmod(g - 2 - FINISH, BLOCKS)
                if t >= 0 and j == 0:
                    pe.wait_ge(s_ft, 2 * (t + 1))
                if t >= 0 and j == 3:
                    pe.wait_ge(s_z_t, ZK * (t + 1))

            def turn(g):
                t, j = divmod(g, BLOCKS)
                pe.wait_ge(s_rows[g], 16 * HALVES * len(new_gathers(j)))
                if g == 0:
                    pe.wait_ge(s_idx, 1)
                if g:
                    turn_free(g)
                for n, i in enumerate(new_gathers(j)):
                    last = pe.transpose(turn_ps[:, n * P:(n + 1) * P], emb[:, t, i, :], ident)
                last.then_inc(s_turn, 1)

            def gram_rows(g):
                pe.wait_ge(s_emb_t, g + 1)
                if g == 0:
                    pe.wait_ge(s_gram, 2)
                if g:
                    pe.wait_ge(s_prod, g)
                for n, _ in enumerate(new_gathers(g % BLOCKS)):
                    last = pe.matmul(gram_ps[:, n * P:(n + 1) * P], emb_t[:, g % 2, n * P:(n + 1) * P], gram[:],
                                     start=True, stop=True)
                last.then_inc(s_gram_rows, 1)

            def spread_rows(g):
                t, j = divmod(g, BLOCKS)
                pe.wait_ge(s_emb_n, g + 1)
                if g == 0:
                    pe.wait_ge(s_spread, len(SPREADS))
                if g:
                    pe.wait_ge(s_spr, HALVES * g)
                mine = [k for k, s in enumerate(SPREADS) if s[0] == j]
                for k in mine:
                    _, i, lo, n = SPREADS[k]
                    last = pe.matmul(spread_ps[:, lo * PROJ:(lo + n) * PROJ], emb_n[:, t % 2, i, :],
                                     spread[:, SPREAD_AT[k]:SPREAD_AT[k + 1], :], start=(k == mine[0]),
                                     stop=(k == mine[-1]), skip_group_check=True)
                last.then_inc(s_spread_ps, 1)

            def project(g, h):
                if g == 0 and h == 0:
                    pe.wait_ge(s_hd, H1 // P)
                    pe.wait_ge(s_bs, 32)
                    pe.wait_ge(s_shift, 2 * HALVES)
                    pe.wait_ge(s_x_n, TILES)
                n = HALVES * g + h
                pe.wait_ge(s_spr, n + 1)
                if n >= 3:
                    pe.wait_ge(s_terms, n - 2)
                pe.matmul(proj_ps[n % 3][:], proj_w[:, h, :], spr[:, g % 2, h, :], start=True, stop=True)\
                  .then_inc(s_proj, 1)

            def pair(g):
                pe.wait_ge(s_terms, HALVES * (g + 1))
                if g == 0:
                    pe.wait_ge(s_xs, 1)
                if g:
                    pe.wait_ge(s_pairs, g)
                for m in range(MB):
                    q, b = divmod(m, MB // 4)
                    last = pe.matmul(pair_ps[PROJ * q:PROJ * (q + 1), b * ZC:(b + 1) * ZC],
                                     terms[:, g % 2, m, 2:SLOTS], terms[:, g % 2, m, 0:ZC], start=True, stop=True,
                                     tile_position=(0, PROJ * q))
                last.then_inc(s_pair_ps, 1)

            def turn_feats(t, part):
                pe.wait_ge(s_feats, t + 1)
                if part == 0:
                    pe.wait_ge(s_emb_t, min(4 * t + FINISH + 2, BLOCKS_ALL))
                if part:
                    pe.wait_ge(s_ft, 2 * t + 1)
                if part == 0:
                    pe.wait_ge(s_packed, t + 1)
                parts = [feats[:, P:2 * P], feats[:, 2 * P:3 * P], packed[:, 0, :], packed[:, 1, :], packed[:, 2, :],
                         feats[:, 0:P]]
                for n, k in enumerate((range(0, 4), range(4, FEATS))[part]):
                    last = pe.transpose(turn_ps[:, n * P:(n + 1) * P], parts[k], ident)
                last.then_inc(s_ft_ps, 1)

            def wide(t, part):
                if part == 0:
                    pe.wait_ge(s_ft, 2 * (t + 1))
                    if t == 0:
                        pe.wait_ge(s_wl_g, PAIR_CHUNKS)
                        pe.wait_ge(s_wl_aux, 1)
                    if t:
                        pe.wait_ge(s_y, t)
                for k in range(part * FEATS // 2, (part + 1) * FEATS // 2):
                    last = pe.matmul(wide_ps[:], feats_t[:, k, :], wl[:, k, :], start=(k == 0), stop=(k == FEATS - 1))
                if part:
                    last.then_inc(s_wide, 1)

            def turn_z(t):
                pe.wait_ge(s_z_n, t + 1)
                pe.wait_ge(s_emb_t, min(4 * t + FINISH + 5, BLOCKS_ALL))
                pe.wait_ge(s_ft, 2 * (t + 1))
                for k in range(ZK):
                    last = pe.transpose(turn_ps[:, k * P:(k + 1) * P], z_n[:, k * P:(k + 1) * P], ident)
                last.then_inc(s_zt_ps, 1)

            def layer1(t):
                if t == 0:
                    pe.wait_ge(s_w12, 32)
                for k in range(ZK):
                    pe.wait_ge(s_z_t, ZK * t + k + 1)
                    for m in range(H1 // P):
                        last = pe.matmul(wide_ps[:, m * P:(m + 1) * P], w1[:, k, m * P:(m + 1) * P], z_t[:, k, :],
                                         start=(k == 0 and m == 0), stop=(k == ZK - 1), skip_group_check=True)
                last.then_inc(s_h1_ps, 1)

            def layer2(t):
                pe.wait_ge(s_h1, t + 1)
                for m in range(H2 // P):
                    for k in range(H1 // P):
                        last = pe.matmul(wide_ps[:, m * P:(m + 1) * P], w2[:, k, m * P:(m + 1) * P], h1_t[:, k, :],
                                         start=(k == 0), stop=(k == H1 // P - 1))
                last.then_inc(s_h2_ps, 1)

            def layer3(t):
                pe.wait_ge(s_h2, t + 1)
                for k in range(H2 // P):
                    last = pe.matmul(wide_ps[0:1, 2 * P:3 * P], v("w3", k), h2_t[:, k, :],
                                     start=(k == 0), stop=(k == H2 // P - 1))
                last.then_inc(s_y_ps, 1)

            turn(0)
            dense_layer1(2)
            sum_x()
            dense_layer1(3)
            for s in range(LAST + 1):
                t, j = divmod(s - FINISH, BLOCKS)
                if s < BLOCKS_ALL:
                    gram_rows(s)
                if s + 1 < BLOCKS_ALL:
                    turn(s + 1)
                if 0 <= s - 2 < BLOCKS_ALL:
                    project(s - 2, 0)
                if 0 <= s - 1 < BLOCKS_ALL:
                    spread_rows(s - 1)
                if 0 <= t < TILES and j == 3:
                    turn_z(t)
                if t >= 1 and j == 0:
                    layer2(t - 1)
                if t >= 0 and j in (1, 2):
                    wide(t, j - 1)
                if s == 3:
                    aux_weights()
                if 0 <= s - 2 < BLOCKS_ALL:
                    project(s - 2, 1)
                if t >= 1 and j == 0:
                    layer3(t - 1)
                if 0 <= t < TILES and j == 0:
                    turn_feats(t, 0)
                if t >= 0 and j == 3:
                    layer1(t)
                if 0 <= s - 3 < BLOCKS_ALL:
                    pair(s - 3)
                if 0 <= t < TILES and j == 0:
                    turn_feats(t, 1)

        @block.scalar
        def _(act):
            act.wait_ge(s_ws_ps, 1)
            act.copy(ws_c[:], gram_ps[:, 0:P]).then_inc(s_ws_c, 1)
            act.wait_ge(s_gram_ps, 1)
            act.wait_ge(s_zeroed_w, 4)
            for h in range(HALVES):
                a = slice(h * D, (h + 1) * D)
                act.mul(gram[a, a], spread_ps[a, a], 1.0 / E).then_inc(s_gram, 1)
            act.wait_ge(s_proj_ps, 1)
            for h in range(HALVES):
                a = slice(h * D, (h + 1) * D)
                act.copy(proj_w[a, h, :], proj_ps[0][a, 0:E]).then_inc(s_proj_w, 1)
            act.wait_ge(s_vec, 16)
            for n in range(TILES // 2):
                act.wait_ge(s_dt_ps, n + 1)
                act.copy(dense_t[:, 2 * n:2 * n + 2, :, :],
                         proj_ps[1 + n][:].rearrange("p (t k b) -> p t k b", t=2, k=DK)).then_inc(s_dt, 1)
            act.wait_ge(s_shift_ps, 1)
            for h, row in enumerate((D, 0)):
                for parity in range(2):
                    act.copy(spr[row:row + 1, parity, h, :].rearrange("o (b p) -> o b p", p=PROJ),
                             pair_ps[row:row + 1, 0:PROJ].unsqueeze(1).to_broadcast([1, BS, PROJ])).then_inc(s_shift, 1)
            act.wait_ge(s_zeroed, 6)
            act.wait_ge(s_x_mv, TILES)
            act.activation(x_std[:], x_mv[:, :, 1], ACT.Sqrt, bias=eps[:]).then_inc(s_x_std, 1)
            def copy_dense_layer1(m):
                act.wait_ge(s_hd_ps, m + 1)
                act.activation(h1_dense[:, m, :], proj_ps[1 + m % 2][:], ACT.Identity, bias=v("b1", m)).then_inc(s_hd, 1)

            copy_dense_layer1(0)
            copy_dense_layer1(1)
            act.wait_ge(s_xt_ps, 1)
            act.activation(x_t[:], wide_ps[:].rearrange("e (t b) -> e t b", b=P), ACT.Identity, bias=v("bd"),
                           scale=v("gd")).then_inc(s_xt, 1)

            def copy_sums():
                act.wait_ge(s_xs_ps, 1)
                act.copy(x_sum[:], pair_ps[:, 0:TILES]).then_inc(s_xs, 1)

            def copy_aux():
                act.wait_ge(s_wl_aux_ps, 1)
                act.copy(wl[:, PAIR_CHUNKS, :], wide_ps[:]).then_inc(s_wl_aux, 1)

            def copy_turned(g):
                act.wait_ge(s_turn, g + 1)
                if g >= 2:
                    act.wait_ge(s_gram_rows, g - 1)
                n = len(new_gathers(g % BLOCKS)) * P
                act.copy(emb_t[:, g % 2, 0:n], turn_ps[:, 0:n]).then_inc(s_emb_t, 1)

            def copy_spread(g):
                act.wait_ge(s_spread_ps, g + 1)
                if g >= 2:
                    act.wait_ge(s_proj, HALVES * (g - 1))
                for h in range(HALVES):
                    a = slice(h * D, (h + 1) * D)
                    act.copy(spr[a, g % 2, h, :], spread_ps[a, :]).then_inc(s_spr, 1)

            def row_std(g):
                act.wait_ge(s_var_c, g + 1)
                if g:
                    act.wait_ge(s_rstd_e, g)
                n = HALVES * len(new_gathers(g % BLOCKS))
                act.activation(std_e[:, 0:n], var_c[:, 0:n], ACT.Sqrt, bias=eps[:]).then_inc(s_std_e, 1)

            def proj_std(g):
                act.wait_ge(s_var_p, HALVES * (g + 1))
                if g:
                    act.wait_ge(s_rstd_p, g)
                act.activation(std_p[:], var_p[:], ACT.Sqrt, bias=eps[:], scale=1.0 / PROJ).then_inc(s_std_p, 1)

            def z_std(t):
                act.wait_ge(s_z_mv, t + 1)
                act.activation(z_std_sb[:], z_mv[:, 1:2], ACT.Sqrt, bias=eps[:]).then_inc(s_z_std, 1)

            def squares(g, h):
                n = HALVES * g + h
                if g:
                    act.wait_ge(s_var_p, n - 1)
                act.wait_ge(s_proj, n + 1)
                act.activation(sq[:, h * BS:(h + 1) * BS, :],
                               proj_ps[n % 3][:].rearrange("e (b p) -> e b p", p=PROJ), ACT.Square).then_inc(s_sq, 1)

            def copy_pairs(g):
                t, j = divmod(g, BLOCKS)
                act.wait_ge(s_pair_ps, g + 1)
                if j == 0 and t:
                    act.wait_ge(s_feats, t)
                n = MB // 4
                act.copy(pairs[:, :, j * n:(j + 1) * n].rearrange("p j b -> p b j"),
                         pair_ps[:, 0:n * ZC].rearrange("p (b j) -> p b j", j=ZC)).then_inc(s_pairs, 1)

            def pack_pairs(t):
                act.wait_ge(s_feats, t + 1)
                if t:
                    act.wait_ge(s_ft_ps, 2 * t)
                grid = feats[:, P:AUX + ZC * PROJ].rearrange("b (j i) -> b j i", i=PROJ)
                act.copy(packed[:, 0, :].rearrange("b (j i) -> b j i", i=16), grid[:, 8:16, 8:24])
                act.copy(packed[:, 1, :].rearrange("b (j i) -> b j i", i=16), grid[:, 16:24, 16:32])
                act.copy(packed[:, 2, :].rearrange("b (a j i) -> b a j i", a=2, i=8),
                         grid[:, 8:, 24:32].rearrange("b (a j) i -> b a j i", j=8)[:, 0::2]).then_inc(s_packed, 1)

            def copy_feats(t, part):
                act.wait_ge(s_ft_ps, 2 * t + part + 1)
                if part == 0 and t:
                    act.wait_ge(s_wide, t)
                a, b = ((0, 4), (4, FEATS))[part]
                act.copy(feats_t[:, a:b, :], turn_ps[:, 0:(b - a) * P].rearrange("p (k b) -> p k b", b=P))\
                   .then_inc(s_ft, 1)

            def scale_z(t):
                act.wait_ge(s_zt_ps, t + 1)
                if t:
                    act.wait_ge(s_h1_ps, t)
                for k in range(ZK):
                    act.activation(z_t[:, k, :], turn_ps[:, k * P:(k + 1) * P], ACT.Identity,
                                   bias=v("bl", k), scale=v("gl", k)).then_inc(s_z_t, 1)

            def relu1(t):
                act.wait_ge(s_h1_sum, t + 1)
                if t:
                    act.wait_ge(s_h2_ps, t)
                act.activation(h1_t[:], h1_sum[:], ACT.Relu).then_inc(s_h1, 1)

            def relu2(t):
                act.wait_ge(s_h2_ps, t + 1)
                if t:
                    act.wait_ge(s_y_ps, t)
                for m in range(H2 // P):
                    last = act.activation(h2_t[:, m, :], wide_ps[:, m * P:(m + 1) * P], ACT.Relu, bias=v("b2", m))
                last.then_inc(s_h2, 1)

            def copy_y(t):
                act.wait_ge(s_y_ps, t + 1)
                src = wide_ps[0:1, 2 * P:3 * P].rearrange("o (h q j b) -> o h j q b", h=2, q=2, j=BLOCKS)
                dst = y_row[0:1, t * P:(t + 1) * P].rearrange("o (h j q b) -> o h j q b", h=2, q=2, j=BLOCKS)
                for h in range(2):
                    last = act.copy(dst[:, h], src[:, h])
                last.then_inc(s_y, 1)

            copy_turned(0)
            copy_dense_layer1(2)
            copy_sums()
            copy_dense_layer1(3)
            for s in range(LAST + 1):
                t, j = divmod(s - FINISH, BLOCKS)
                if 0 <= t < TILES and j == 0:
                    pack_pairs(t)
                if s + 1 < BLOCKS_ALL:
                    copy_turned(s + 1)
                if 0 <= s - 2 < BLOCKS_ALL:
                    squares(s - 2, 0)
                if s < BLOCKS_ALL:
                    row_std(s)
                if 0 <= s - 1 < BLOCKS_ALL:
                    copy_spread(s - 1)
                if t >= 0 and j == 3:
                    scale_z(t)
                if t >= 1 and j == 0:
                    relu2(t - 1)
                if 0 <= s - 2 < BLOCKS_ALL:
                    squares(s - 2, 1)
                if s == 3:
                    copy_aux()
                if t >= 1 and j == 0:
                    copy_y(t - 1)
                if 0 <= t < TILES and j == 0:
                    copy_feats(t, 0)
                if t >= 0 and j == 2:
                    z_std(t)
                if 0 <= s - 2 < BLOCKS_ALL:
                    proj_std(s - 2)
                if 0 <= s - 3 < BLOCKS_ALL:
                    copy_pairs(s - 3)
                if t >= 0 and j == 3:
                    relu1(t)
                if 0 <= t < TILES and j == 0:
                    copy_feats(t, 1)

        @block.vector
        def _(dve):
            dve.memset(gram[:], 0.0).then_inc(s_zeroed_w, 1)
            dve.memset(proj_w[:], 0.0).then_inc(s_zeroed_w, 1)
            dve.memset(spr[D:P, :, 0, :], 0.0).then_inc(s_zeroed_w, 1)
            dve.memset(spr[0:D, :, 1, :], 0.0).then_inc(s_zeroed_w, 1)
            dve.wait_ge(s_ids, 32)
            dve.tensor_tensor(ids_sum[:], ids_raw[:], ids_off[:], ALU.add).then_inc(s_ids_sum, 1)
            dve.wait_ge(s_ids_t, 1)
            dve.tensor_copy(idx[:], turn_ps[:, 0:TILES * HALVES * GATHERS]).then_inc(s_idx, 1)
            dve.wait_ge(s_vec, 16)
            dve.wait_ge(s_ws_c, 1)
            dve.tensor_scalar(ws_cg[:], ws_c[:], v("gs"), None, ALU.mult).then_inc(s_ws_cg, 1)
            dve.wait_ge(s_wsi, 16)
            dve.tensor_reduce(wsi_mean[:], wsi_raw[:], AX.X, ALU.add).then_inc(s_wsi_mean, 1)
            dve.wait_ge(s_wsi_mean, 1)
            dve.tensor_scalar(wsi_m[:], wsi_mean[:], 1.0 / PROJ, None, ALU.mult).then_inc(s_wsi_m, 1)
            dve.wait_ge(s_wsi_m, 1)
            dve.tensor_tensor(wsi_c[:], wsi_raw[:], wsi_m[:].unsqueeze(2).to_broadcast([P, GATHERS, PROJ]),
                              ALU.subtract).then_inc(s_wsi_c, 1)
            dve.wait_ge(s_con, 16)
            dve.wait_ge(s_wsi_c, 1)
            for k, (_, i, _, n) in enumerate(SPREADS):
                mask = c("spread")[:, SPREAD_AT[k]:SPREAD_AT[k + 1]]
                dve.tensor_tensor(spread[:, SPREAD_AT[k]:SPREAD_AT[k + 1], :],
                                  mask.unsqueeze(2).to_broadcast([P, n, PROJ]),
                                  wsi_c[:, i:i + 1, :].to_broadcast([P, n, PROJ]), ALU.mult).then_inc(s_spread, 1)

            dve.wait_ge(s_x_ps, 1)
            for t in range(TILES):
                dve.bn_stats(x_stats[:, t, :], proj_ps[0][:, t * P:(t + 1) * P]).then_inc(s_x_stats, 1)
            for t in range(TILES):
                dve.wait_ge(s_x_stats, t + 1)
                dve.bn_aggr(x_mv[:, t, :], x_stats[:, t, :]).then_inc(s_x_mv, 1)
            dve.wait_ge(s_x_std, 1)
            dve.reciprocal(x_rstd[:], x_std[:]).then_inc(s_x_rstd, 1)
            dve.wait_ge(s_x_rstd, 1)
            for t in range(TILES):
                dve.tensor_scalar(x_n[:, t, :], proj_ps[0][:, t * P:(t + 1) * P], x_mv[:, t, 0:1], x_rstd[:, t:t + 1],
                                  ALU.subtract, ALU.mult).then_inc(s_x_n, 1)

            def pair_weights():
                a, b = VEC["gj"]
                dve.tensor_tensor(gj0[:], vec[:, a:b], c("not_x"), ALU.mult).then_inc(s_pair_v, 1)
                a, b = VEC["bj"]
                dve.tensor_tensor(bj[:], vec[:, a:b], c("not_x"), ALU.mult).then_inc(s_pair_v, 1)
                dve.wait_ge(s_pair_v, 2)
                dve.tensor_tensor(gj[:], gj0[:], c("is_x"), ALU.add).then_inc(s_pair_v, 1)
                dve.wait_ge(s_pair_v, 3)
                a, b = VEC["gi"]
                dve.tensor_tensor(gij[:], vec[:, a:b], gj[:], ALU.mult).then_inc(s_pair_v, 1)
                dve.wait_ge(s_zeroed, 6)
                for k in range(PAIR_CHUNKS):
                    pick_i = c("pick_i")[:, k * PROJ:(k + 1) * PROJ]
                    pick_j = c("pick_j")[:, k * PROJ:(k + 1) * PROJ]
                    dve.tensor_scalar(aux_i[:, k, :], pick_i, v("gi", k), bj[:, k:k + 1], ALU.mult, ALU.mult)
                    dve.tensor_scalar(aux_j[:, k, :], pick_j, v("bi", k), gj[:, k:k + 1], ALU.mult, ALU.mult)\
                       .then_inc(s_aux_ij, 1)
                dve.wait_ge(s_aux_ij, PAIR_CHUNKS)
                a, b = VEC["bi"]
                dve.tensor_tensor(aux_w[:, :, AUX:P], aux_i[:], aux_j[:], ALU.add).then_inc(s_aux_w, 1)
                dve.tensor_tensor(aux_w[:, :, SX], vec[:, a:b], c("is_x"), ALU.mult).then_inc(s_aux_w, 1)
                dve.scalar_tensor_tensor(aux_w[:, :, ONE], vec[:, a:b], float(E), bj[:], ALU.mult, ALU.mult)\
                   .then_inc(s_aux_w, 1)
            def scale_wl():
                dve.wait_ge(s_pair_v, 4)
                dve.wait_ge(s_wl_aux_ps, 1)
                for k in range(PAIR_CHUNKS):
                    dve.tensor_scalar(wl[:, k, :], wl[:, k, :], gij[:, k:k + 1], None, ALU.mult).then_inc(s_wl_g, 1)

            def row_variances(g):
                t, j = divmod(g, BLOCKS)
                rows = new_gathers(j)
                w = len(rows)
                e = emb[:, t, rows[0]:rows[0] + w, :]
                dve.wait_ge(s_gram_rows, g + 1)
                dve.tensor_tensor(prod[:, 0:w * P].rearrange("p (i c) -> p i c", c=P),
                                  gram_ps[:, 0:w * P].rearrange("p (i c) -> p i c", c=P), e, ALU.mult)\
                   .then_inc(s_prod, 1)
                dve.wait_ge(s_prod, g + 1)
                dve.tensor_reduce(var_e[:, 0:2 * w], prod[:, 0:w * P].rearrange("p (n d) -> p n d", d=D), AX.X,
                                  ALU.add).then_inc(s_var_e, 1)
                dve.wait_ge(s_var_e, g + 1)
                if g:
                    dve.wait_ge(s_std_e, g)
                dve.tensor_scalar(var_c[:, 0:2 * w], var_e[:, 0:2 * w], 0.0, None, ALU.max).then_inc(s_var_c, 1)

            def normalise_rows(g):
                t, j = divmod(g, BLOCKS)
                rows = new_gathers(j)
                w = len(rows)
                e = emb[:, t, rows[0]:rows[0] + w, :]
                dve.wait_ge(s_std_e, g + 1)
                dve.reciprocal(rstd_e[:, 0:2 * w], std_e[:, 0:2 * w]).then_inc(s_rstd_e, 1)
                dve.wait_ge(s_rstd_e, g + 1)
                if t >= 2:
                    dve.wait_ge(s_spread_ps, (t - 1) * BLOCKS)
                dve.tensor_tensor(emb_n[:, t % 2, rows[0]:rows[0] + w, :].rearrange("p i (h d) -> p (i h) d", d=D),
                                  e.rearrange("p i (h d) -> p (i h) d", d=D),
                                  rstd_e[:, 0:2 * w].unsqueeze(2).to_broadcast([P, 2 * w, D]), ALU.mult)\
                   .then_inc(s_emb_n, 1)

            def proj_variances(g, h):
                dve.wait_ge(s_sq, HALVES * g + h + 1)
                if g:
                    dve.wait_ge(s_std_p, g)
                a = slice(h * BS, (h + 1) * BS)
                dve.tensor_reduce(var_p[:, a], sq[:, a, :], AX.X, ALU.add).then_inc(s_var_p, 1)

            def normalise_proj(g):
                t, j = divmod(g, BLOCKS)
                if g >= 2:
                    dve.wait_ge(s_pair_ps, g - 1)
                if g == 0:
                    dve.wait_ge(s_xt, 1)
                x = x_t[:, t, :].rearrange("e (q j b) -> e q j b", q=4, j=BLOCKS)[:, :, j, :]
                dve.tensor_copy(terms[:, g % 2, :, 1].rearrange("e (q b) -> e q b", q=4), x)
                dve.wait_ge(s_std_p, g + 1)
                dve.reciprocal(rstd_p[:], std_p[:]).then_inc(s_rstd_p, 1)
                dve.wait_ge(s_rstd_p, g + 1)
                for h in range(HALVES):
                    a = slice(h * BS, (h + 1) * BS)
                    dve.tensor_tensor(terms[:, g % 2, a, 2:SLOTS],
                                      proj_ps[(HALVES * g + h) % 3][:].rearrange("e (b p) -> e b p", p=PROJ),
                                      rstd_p[:, a].unsqueeze(2).to_broadcast([E, BS, PROJ]), ALU.mult)\
                       .then_inc(s_terms, 1)

            def turn_pairs(t):
                dve.wait_ge(s_pairs, BLOCKS * (t + 1))
                if t:
                    dve.wait_ge(s_ft_ps, 2 * t)
                dve.tensor_copy(feats[:, SX:SX + 1], x_sum[:, t:t + 1])
                dve.transpose(feats[:, AUX:AUX + ZC * PROJ], pairs[:].rearrange("p j b -> p (j b)")).then_inc(s_feats, 1)

            def z_variances(t):
                dve.wait_ge(s_wide, t + 1)
                dve.bn_stats(z_stats[:], wide_ps[:]).then_inc(s_z_stats, 1)
                dve.wait_ge(s_z_stats, t + 1)
                dve.bn_aggr(z_mv[:], z_stats[:]).then_inc(s_z_mv, 1)

            def normalise_z(t):
                dve.wait_ge(s_z_std, t + 1)
                dve.reciprocal(z_rstd[:], z_std_sb[:]).then_inc(s_z_rstd, 1)
                dve.wait_ge(s_z_rstd, t + 1)
                if t:
                    dve.wait_ge(s_zt_ps, t)
                dve.tensor_scalar(z_n[:], wide_ps[:, 0:DIMS], z_mv[:, 0:1], z_rstd[:], ALU.subtract, ALU.mult)\
                   .then_inc(s_z_n, 1)

            def add_dense(t):
                dve.wait_ge(s_h1_ps, t + 1)
                if t == 0:
                    dve.wait_ge(s_hd, H1 // P)
                if t:
                    dve.wait_ge(s_h1, t)
                dve.tensor_tensor(h1_sum[:], wide_ps[:].rearrange("p (m b) -> p m b", b=P),
                                  h1_dense[:, :, t * P:(t + 1) * P], ALU.add).then_inc(s_h1_sum, 1)

            for s in range(LAST + 1):
                t, j = divmod(s - FINISH, BLOCKS)
                if 0 <= s - 3 < BLOCKS_ALL:
                    proj_variances(s - 3, 1)
                if t >= 0 and j == 3:
                    normalise_z(t)
                if 0 <= t < TILES and j == 0:
                    turn_pairs(t)
                if s < BLOCKS_ALL:
                    row_variances(s)
                if 0 <= s - 3 < BLOCKS_ALL:
                    normalise_proj(s - 3)
                if s < BLOCKS_ALL:
                    normalise_rows(s)
                if 0 <= s - 2 < BLOCKS_ALL:
                    proj_variances(s - 2, 0)
                if s == 1:
                    pair_weights()
                if s == 4:
                    scale_wl()
                if t >= 0 and j == 2:
                    z_variances(t)
                if t >= 0 and j == 3:
                    add_dense(t)


def layout(inputs):
    tables = [np.asarray(inputs[f"tbl_{k}"]) for k in range(NT)]
    get = {k: np.asarray(a) for k, a in inputs.items() if not k.startswith("tbl_")}
    a = {"table": np.concatenate(tables, axis=0)}
    first = np.concatenate([[0], np.cumsum([x.shape[0] for x in tables])])[:NT]
    n = TILES * HALVES * GATHERS
    a["ids"] = get["ids"].reshape(n, P)
    a["offsets"] = np.tile(first, BATCH).reshape(n, P).astype(np.float32)
    a["dense"] = get["r_dense_t"].reshape(TILES, 2, BLOCKS, 2, 8, DENSE).transpose(0, 1, 3, 2, 4, 5)\
        .reshape(TILES, P, DENSE)
    a["wd_t"] = get["L0_rec_Wd"].T
    a["ws2"] = np.concatenate([get["L0_rec_Ws"]] * 2, axis=1)
    a["wsi_rep"] = np.tile(get["L0_rec_Wsi"].T, (HALF, 1)).reshape(GATHERS, P, PROJ)
    a["bs_row"] = get["L0_rec_bs"].reshape(1, E)
    chunks = pair_chunks()
    wl_t = get["L0_rec_Wl"].T
    packed = np.zeros((PAIR_CHUNKS, P, MAXD), np.float32)
    con = np.zeros((P, CONS), np.float32)
    vec = np.zeros((P, VECS), np.float32)

    def cols(name, k=0, w=1):
        return slice(CON[name][0] + k * w, CON[name][0] + (k + 1) * w)

    for k, chunk in enumerate(chunks):
        i = np.array([x[1] for x in chunk])
        j = np.array([x[0] for x in chunk])
        live = i >= j
        packed[k, live] = wl_t[(i * (i + 1) // 2 + j)[live]]
        con[np.arange(P), CON["pick_i"][0] + k * PROJ + i] = 1.0
        y = j >= 1
        con[np.arange(P)[y], CON["pick_j"][0] + k * PROJ + j[y] - 1] = 1.0
        con[:, CON["is_x"][0] + k] = ~y
        con[:, CON["not_x"][0] + k] = y
        for name, src, at in (("gi", "gsi", i), ("bi", "bsi", i), ("gj", "gsi", np.maximum(j - 1, 0)),
                              ("bj", "bsi", np.maximum(j - 1, 0))):
            vec[:, VEC[name][0] + k] = get[f"L0_rec_{src}"][at]
    a["wl_t"] = packed.reshape(PAIR_CHUNKS * P, MAXD)
    con[:, CON["ident"][0]:CON["ident"][1]] = np.eye(P)
    con[:, CON["centre"][0]:CON["centre"][1]] = np.eye(P) - 1.0 / P
    for k, (j, i, lo, m) in enumerate(SPREADS):
        sample = (i * P + np.arange(P)) // NT - j * BS - lo
        ok = (sample >= 0) & (sample < m)
        con[np.arange(P)[ok], CON["spread"][0] + SPREAD_AT[k] + sample[ok]] = 1.0
    for name, src, w in (("gs", "L0_rec_gs", 1), ("gd", "L0_rec_gd", 1), ("bd", "L0_rec_bd", 1),
                         ("gl", "L0_rec_gl", ZK), ("bl", "L0_rec_bl", ZK), ("b1", "b_top1", H1 // P),
                         ("b2", "b_top2", H2 // P), ("w3", "W_top3", H2 // P)):
        vec[:, VEC[name][0]:VEC[name][1]] = get[src].reshape(-1, P)[:w].T
    a["consts"], a["vecs"] = con, vec
    w_top1 = get["W_top1"]
    a["w1_t"] = np.concatenate([w_top1[0:DIMS], w_top1[MAXD:]], axis=0)
    a["w2_t"] = get["W_top2"]
    return a


_INS = ["table", "ids", "offsets", "dense", "consts", "vecs", "bs_row", "wd_t", "ws2", "wsi_rep", "wl_t", "w1_t", "w2_t"]


def kernel(**inputs):
    import concourse.bacc as bacc
    from concourse.bass_utils import run_bass_kernel_spmd

    nc = bacc.Bacc("TRN2", target_bir_lowering=False, num_devices=1)
    arrays, args = {}, []
    for name, a in layout(inputs).items():
        arrays[f"in_{name}"] = np.ascontiguousarray(a)
    for name in _INS:
        a = arrays[f"in_{name}"]
        args.append(nc.dram_tensor(f"in_{name}", a.shape, mybir.dt.from_np(a.dtype), kind="ExternalInput").ap())
    out = nc.dram_tensor("out_y", (1, BATCH), F32, kind="ExternalOutput").ap()
    build(nc, *args, out)
    r = run_bass_kernel_spmd(nc, [arrays], core_ids=[0])
    return r.results[0]["out_y"].reshape(BATCH, 1)
```

```python
from contextlib import ExitStack

import numpy as np

import concourse.bass as bass
from concourse import mybir

ALU = mybir.AluOpType
ACT = mybir.ActivationFunctionType
AX = mybir.AxisListType
F32 = mybir.dt.float32
I32 = mybir.dt.int32
F32R = mybir.dt.float32r

P = 128
BATCH = 512
TILES = BATCH // P
NT = 26
D = 64
E = 128
PROJ = 32
HALVES = 2
HALF = P // HALVES
GATHERS = HALF * NT // P
BLOCKS = 4
BS = HALF // BLOCKS
MB = HALVES * BS
COLS = BS * PROJ
SLOTS = PROJ + 2
ZC = PROJ + 1
DENSE = 256
DK = DENSE // P
MAXD = 512
DIMS = 384
ZK = DIMS // P
H1 = 512
H2 = 256
EPS = 1e-5
CHUNKS = 5
SUM_AT = ((2, 112, 0), (3, 48, 16))
SX_AT = (4, 64)
ONE_AT = (4, 65)
CLOCK_PRODUCTS = 2


def new_gathers(j):
    first = -(-j * BS * NT // P)
    return range(first, -(-(j + 1) * BS * NT // P))


def block_gathers(j):
    out = []
    for i in range(GATHERS):
        lo = max(i * P // NT, j * BS)
        hi = min(((i + 1) * P - 1) // NT, (j + 1) * BS - 1)
        if lo <= hi:
            out.append((i, lo - j * BS, hi - lo + 1))
    return out


SPREADS = [(j, i, lo, n) for j in range(BLOCKS) for i, lo, n in block_gathers(j)]
SPREAD_AT = np.concatenate([[0], np.cumsum([n for _, _, _, n in SPREADS])]).astype(int)


def pair_chunks():
    def rect(j0, j1, i0, i1):
        return [(j, i) for j in range(j0, j1) for i in range(i0, i1)]
    sums = [None] * 16
    return [rect(0, 4, 0, 32), rect(4, 8, 0, 32),
            rect(8, 12, 8, 24) + rect(12, 16, 12, 24) + sums,
            rect(20, 24, 20, 32) + sums + rect(16, 20, 16, 32),
            rect(8, 16, 24, 32) + sums + rect(24, 28, 24, 32) + rect(28, 32, 28, 32)]


def columns(widths):
    at, out = 0, {}
    for name, w in widths:
        out[name] = (at, at + w)
        at += w
    return out, at


VEC, VECS = columns([("gs", 1), ("gd", 1), ("bd", 1), ("gl", ZK), ("bl", ZK), ("b1", H1 // P), ("b2", H2 // P),
                     ("w3", H2 // P), ("gi", 5), ("bi", 5), ("gj", 5), ("bj", 5)])
CON, CONS = columns([("ident", P), ("centre", P), ("pick_i", 5 * PROJ), ("pick_j", 5 * PROJ), ("is_x", CHUNKS),
                     ("not_x", 5), ("spread", int(SPREAD_AT[-1])), ("sum_rows", CHUNKS), ("high_w", 1), ("low_w", 1), ("high_v", 1),
                     ("low_v", 1)])


def build(nc, table, ids, offsets, dense, consts, vecs, bs_rep, wd_t, ws2, wsi_rep, wl_t, w1_t, w2_t, out):
    with ExitStack() as ctx:
        def sb(name, shape, dt=F32):
            return ctx.enter_context(nc.sbuf_tensor(name, shape, dt))

        def sem(name):
            return ctx.enter_context(nc.semaphore(name))

        banks = [ctx.enter_context(nc.psum_tensor(f"bank{i}", [P, 512], F32)) for i in range(8)]
        turn_ps, gram_ps, spread_ps, wide_ps, pair_ps = banks[0:3] + banks[6:8]
        proj_ps = banks[3:6]

        con = sb("con", [P, CONS])
        vec = sb("vec", [P, VECS])
        ids_raw = sb("ids_raw", [P, TILES * HALVES * GATHERS], I32)
        ids_off = sb("ids_off", [P, TILES * HALVES * GATHERS], I32)
        idx = sb("idx", [P, TILES * HALVES * GATHERS], I32)
        ws_sb = sb("ws_sb", [E, 2 * D])
        ws_c = sb("ws_c", [E, 2 * D])
        ws_cg = sb("ws_cg", [E, 2 * D])
        gram = sb("gram", [P, P])
        proj_high = sb("proj_high", [P, E], F32R)
        proj_low = sb("proj_low", [P, HALVES, E], F32R)
        bs_sb = sb("bs_sb", [P, E])
        bs_high = sb("bs_high", [P, E], F32R)
        bs_low = sb("bs_low", [P, E])
        bs_part = sb("bs_part", [P, E])
        sum_high = sb("sum_high", [P, PROJ], F32R)
        sum_low = sb("sum_low", [P, PROJ])
        sum_part = sb("sum_part", [P, PROJ])
        sum_parts = sb("sum_parts", [P, PROJ])
        wsi_raw = sb("wsi_raw", [P, GATHERS, PROJ])
        wsi_mean = sb("wsi_mean", [P, GATHERS])
        wsi_m = sb("wsi_m", [P, GATHERS])
        wsi_c = sb("wsi_c", [P, GATHERS, PROJ])
        spread = sb("spread", [P, int(SPREAD_AT[-1]), PROJ])
        wd = sb("wd", [P, DK, E])
        dense_sb = sb("dense_sb", [P, TILES, DENSE])
        dense_t = sb("dense_t", [P, TILES, DK, P])
        wl = sb("wl", [P, CHUNKS, MAXD])
        w1 = sb("w1", [P, ZK + DK, H1])
        w2 = sb("w2", [P, H1 // P, H2])
        gj = sb("gj", [P, CHUNKS])
        gj0 = sb("gj0", [P, CHUNKS])
        bj = sb("bj", [P, CHUNKS])
        gij = sb("gij", [P, CHUNKS])
        aux_w = sb("aux_w", [P, CHUNKS, P])
        aux_i = sb("aux_i", [P, CHUNKS, PROJ])
        aux_j = sb("aux_j", [P, CHUNKS, PROJ])
        ones = sb("ones", [P, P])
        eps = sb("eps", [P, 1])
        x_stats = sb("x_stats", [P, TILES, 6])
        x_mv = sb("x_mv", [P, TILES, 2])
        x_std = sb("x_std", [P, TILES])
        x_rstd = sb("x_rstd", [P, TILES])
        x_n = sb("x_n", [P, TILES, E])
        x_t = sb("x_t", [E, TILES, P])
        x_sum = sb("x_sum", [P, TILES])
        emb = sb("emb", [P, TILES, GATHERS, HALVES * D])
        emb_t = sb("emb_t", [P, 2, 4 * P])
        prod = sb("prod", [P, 4 * P])
        var_e = sb("var_e", [P, 8])
        var_c = sb("var_c", [P, 8])
        std_e = sb("std_e", [P, 8])
        rstd_e = sb("rstd_e", [P, 8])
        emb_n = sb("emb_n", [P, 2, GATHERS, HALVES * D])
        spr = sb("spr", [P, 2, HALVES, 2, COLS], F32R)
        sq = sb("sq", [E, MB, PROJ])
        var_p = sb("var_p", [E, MB])
        std_p = sb("std_p", [E, MB])
        rstd_p = sb("rstd_p", [E, MB])
        terms = sb("terms", [E, 2, MB, SLOTS])
        pairs = sb("pairs", [P, ZC, PROJ])
        feats = sb("feats", [P, ZC * PROJ])
        packed = sb("packed", [P, 3, P])
        feats_t = sb("feats_t", [P, CHUNKS, P])
        z_stats = sb("z_stats", [P, 6])
        z_mv = sb("z_mv", [P, 2])
        z_std_sb = sb("z_std_sb", [P, 1])
        z_rstd = sb("z_rstd", [P, 1])
        z_shift = sb("z_shift", [P, 1])
        z_n = sb("z_n", [P, DIMS])
        z_t = sb("z_t", [P, ZK, P])
        h1_dense = sb("h1_dense", [P, H1 // P, BATCH])
        h1_sum = sb("h1_sum", [P, H1 // P, P])
        h1_t = sb("h1_t", [P, H1 // P, P])
        h2_t = sb("h2_t", [P, H2 // P, P])
        y_row = sb("y_row", [1, BATCH])

        s_ids, s_con, s_vec, s_ws, s_wsi, s_bs, s_dense, s_wd, s_wl, s_w12, s_out = map(sem, (
            "s_ids", "s_con", "s_vec", "s_ws", "s_wsi", "s_bs", "s_dense", "s_wd", "s_wl", "s_w12", "s_out"))
        s_rows = [sem(f"s_rows{g}") for g in range(TILES * BLOCKS)]
        s_idx, s_ident, s_warm = map(sem, ("s_idx", "s_ident", "s_warm"))
        s_zeroed_w, s_w1d, s_hd_ps, s_hd, s_h1_sum = map(sem, ("s_zeroed_w", "s_w1d", "s_hd_ps", "s_hd", "s_h1_sum"))
        s_zeroed, s_ws_ps, s_ws_c, s_gram_ps, s_gram = map(sem, ("s_zeroed", "s_ws_ps", "s_ws_c", "s_gram_ps", "s_gram"))
        s_ws_cg, s_proj_ps, s_proj_w = map(sem, ("s_ws_cg", "s_proj_ps", "s_proj_w"))
        s_wsi_mean, s_wsi_m, s_wsi_c, s_spread, s_shift_ps, s_shift = map(sem, (
            "s_wsi_mean", "s_wsi_m", "s_wsi_c", "s_spread", "s_shift_ps", "s_shift"))
        s_proj_low, s_bs_high, s_bs_low, s_bs_part, s_proj_bs, s_sum_high, s_sum_low, s_sum_part, s_sum_parts = map(
            sem, ("s_proj_low", "s_bs_high", "s_bs_low", "s_bs_part", "s_proj_bs", "s_sum_high", "s_sum_low",
                  "s_sum_part", "s_sum_parts"))
        s_pair_v, s_aux_ij, s_aux_w, s_wl_aux_ps, s_wl_aux, s_wl_g = map(sem, (
            "s_pair_v", "s_aux_ij", "s_aux_w", "s_wl_aux_ps", "s_wl_aux", "s_wl_g"))
        s_dt_ps, s_dt, s_x_ps, s_x_stats, s_x_mv, s_x_std, s_x_rstd, s_x_n, s_xt_ps, s_xt, s_xs_ps, s_xs = map(sem, (
            "s_dt_ps", "s_dt", "s_x_ps", "s_x_stats", "s_x_mv", "s_x_std", "s_x_rstd", "s_x_n", "s_xt_ps", "s_xt",
            "s_xs_ps", "s_xs"))
        s_turn, s_emb_t, s_gram_rows, s_prod, s_var_e, s_var_c, s_std_e, s_rstd_e, s_emb_n = map(sem, (
            "s_turn", "s_emb_t", "s_gram_rows", "s_prod", "s_var_e", "s_var_c", "s_std_e", "s_rstd_e", "s_emb_n"))
        s_spread_ps, s_spr_high, s_spr, s_proj, s_sq, s_var_p, s_std_p, s_rstd_p, s_terms, s_pair_ps, s_pairs = map(sem, (
            "s_spread_ps", "s_spr_high", "s_spr", "s_proj", "s_sq", "s_var_p", "s_std_p", "s_rstd_p", "s_terms",
            "s_pair_ps", "s_pairs"))
        s_packed = sem("s_packed")
        s_feats, s_ft_ps, s_ft, s_wide, s_z_stats, s_z_mv, s_z_std, s_z_rstd, s_z_shift, s_z_n, s_zt_ps, s_z_t = map(sem, (
            "s_feats", "s_ft_ps", "s_ft", "s_wide", "s_z_stats", "s_z_mv", "s_z_std", "s_z_rstd", "s_z_shift", "s_z_n", "s_zt_ps",
            "s_z_t"))
        s_h1_ps, s_h1, s_h2_ps, s_h2, s_y_ps, s_y = map(sem, ("s_h1_ps", "s_h1", "s_h2_ps", "s_h2", "s_y_ps", "s_y"))

        def c(name):
            a, b = CON[name]
            return con[:, a:b]

        def v(name, k=0):
            a = VEC[name][0] + k
            return vec[:, a:a + 1]

        ident = c("ident")
        BLOCKS_ALL = TILES * BLOCKS
        STEPS = range(-1, BLOCKS_ALL + 9)

        def blocks(n):
            return range(n, n + 1) if 0 <= n < BLOCKS_ALL else ()

        def tiles(n):
            return range(n // BLOCKS, n // BLOCKS + 1) if n % BLOCKS == 0 and 0 <= n < BLOCKS_ALL else ()

        block = ctx.enter_context(nc.Block())

        @block.sync
        def _(sp):
            sp.dma_start(ids_raw[:], ids).then_inc(s_ids, 16)
            sp.dma_start(ids_off[:], offsets).then_inc(s_ids, 16)
            sp.dma_start(ws_sb[:], ws2).then_inc(s_ws, 16)
            sp.dma_start(con[:, 0:2 * P], consts[:, 0:2 * P]).then_inc(s_ident, 16)
            sp.dma_start(con[:, 2 * P:], consts[:, 2 * P:]).then_inc(s_con, 16)
            sp.dma_start(wsi_raw[:], wsi_rep.rearrange("i p c -> p i c")).then_inc(s_wsi, 16)
            sp.dma_start(vec[:], vecs).then_inc(s_vec, 16)
            sp.dma_start(dense_sb[:], dense.rearrange("t p c -> p t c")).then_inc(s_dense, 16)
            sp.dma_start(wd[:], wd_t.rearrange("(k p) e -> p k e", p=P)).then_inc(s_wd, 16)
            sp.dma_start(w1[:, ZK:ZK + DK, :], w1_t[DIMS:, :].rearrange("(k p) o -> p k o", p=P)).then_inc(s_w1d, 16)
            sp.dma_start(bs_sb[:], bs_rep).then_inc(s_bs, 16)
            sp.dma_start(wl[:], wl_t.rearrange("(k p) o -> p k o", p=P)).then_inc(s_wl, 16)
            sp.wait_ge(s_rows[2], 16 * HALVES * len(new_gathers(2)))
            sp.dma_start(w1[:, 0:ZK, :], w1_t[0:DIMS, :].rearrange("(k p) o -> p k o", p=P)).then_inc(s_w12, 16)
            sp.dma_start(w2[:], w2_t.rearrange("(k p) o -> p k o", p=P)).then_inc(s_w12, 16)
            sp.wait_ge(s_y, TILES)
            sp.dma_start(out, y_row[:]).then_inc(s_out, 16)
            sp.wait_ge(s_out, 16)

        @block.gpsimd
        def _(pool):
            pool.memset(ones[:], 1.0).then_inc(s_zeroed, 1)
            pool.memset(eps[:], EPS).then_inc(s_zeroed, 1)
            pool.memset(terms[:, :, :, 0:1], 1.0).then_inc(s_zeroed, 1)
            pool.memset(packed[:, 2, ONE_AT[1]:ONE_AT[1] + 1], 1.0).then_inc(s_zeroed, 1)
            pool.memset(packed[:, 2, ONE_AT[1] + 1:SX_AT[1] + 16], 0.0).then_inc(s_zeroed, 1)
            pool.memset(aux_w[:], 0.0).then_inc(s_zeroed, 1)
            pool.wait_ge(s_idx, 1)
            for t in range(TILES):
                for j in range(BLOCKS):
                    for i in new_gathers(j):
                        for h in range(HALVES):
                            at = (t * HALVES + h) * GATHERS + i
                            pool.indirect_dma_start(
                                emb[:, t, i, h * D:(h + 1) * D], None, table,
                                bass.IndirectOffsetOnAxis(ap=idx[:, at:at + 1], axis=0),
                            ).then_inc(s_rows[t * BLOCKS + j], 16)

        @block.tensor
        def _(pe):
            pe.wait_ge(s_ident, 16)
            pe.wait_ge(s_ws, 16)
            pe.matmul(gram_ps[:, 0:P], c("centre"), ws_sb[:], start=True, stop=True).then_inc(s_ws_ps, 1)
            pe.wait_ge(s_ws_c, 1)
            pe.matmul(spread_ps[:, 0:P], ws_c[:], ws_c[:], start=True, stop=True).then_inc(s_gram_ps, 1)
            pe.wait_ge(s_ws_cg, 1)
            pe.transpose(proj_ps[0][:, 0:P], ws_cg[:], ident).then_inc(s_proj_ps, 1)
            pe.wait_ge(s_zeroed, 6)
            pe.wait_ge(s_wsi_c, 1)
            pe.matmul(pair_ps[:, 0:PROJ], ones[0:NT, :], wsi_c[0:NT, 0, :], start=True, stop=True)\
              .then_inc(s_shift_ps, 1)
            pe.wait_ge(s_dense, 16)
            pe.wait_ge(s_proj_low, HALVES)
            for t in range(TILES):
                bank, at = proj_ps[1 + t // 2], (t % 2) * DK * P
                for k in range(DK):
                    last = pe.transpose(bank[:, at + k * P:at + (k + 1) * P], dense_sb[:, t, k * P:(k + 1) * P], ident)
                if t % 2:
                    last.then_inc(s_dt_ps, 1)
            pe.wait_ge(s_wd, 16)
            for t in range(TILES):
                if t % 2 == 0:
                    pe.wait_ge(s_dt, t // 2 + 1)
                for k in range(DK):
                    last = pe.matmul(proj_ps[0][:, t * P:(t + 1) * P], dense_t[:, t, k, :], wd[:, k, :],
                                     start=(k == 0), stop=(k == DK - 1))
            last.then_inc(s_x_ps, 1)

            def dense_layer1(m):
                pe.wait_ge(s_w1d, 16)
                if m >= 2:
                    pe.wait_ge(s_hd, m - 1)
                for k in range(DK):
                    last = pe.matmul(proj_ps[1 + m % 2][:], w1[:, ZK + k, m * P:(m + 1) * P], dense_t[:, :, k, :],
                                     start=(k == 0), stop=(k == DK - 1))
                last.then_inc(s_hd_ps, 1)

            reader = {"turn_ps": (s_gram, 2), "wide_ps": (s_xt, 1)}

            def sum_x():
                pe.wait_ge(s_xt, 1)
                pe.wait_ge(s_sum_low, 1)
                for t in range(TILES):
                    last = pe.matmul(pair_ps[:, t:t + 1], x_t[:, t, :], ones[:, 0:1], start=True, stop=True)
                last.then_inc(s_xs_ps, 1)

            def aux_weights():
                pe.wait_ge(s_wl, 16)
                pe.wait_ge(s_aux_w, 4)
                pe.wait_ge(*reader["wide_ps"])
                reader["wide_ps"] = (s_wl_aux, 3)
                for k in range(CHUNKS):
                    last = pe.matmul(wide_ps[:], aux_w[:, k, :], wl[:, k, :], start=(k == 0),
                                     stop=(k == CHUNKS - 1))
                last.then_inc(s_wl_aux_ps, 1)

            def turn(g):
                t, j = divmod(g, BLOCKS)
                pe.wait_ge(s_rows[g], 16 * HALVES * len(new_gathers(j)))
                pe.wait_ge(*reader["turn_ps"])
                reader["turn_ps"] = (s_emb_t, g + 1)
                for n, i in enumerate(new_gathers(j)):
                    last = pe.transpose(turn_ps[:, n * P:(n + 1) * P], emb[:, t, i, :], ident)
                last.then_inc(s_turn, 1)

            def gram_rows(g):
                pe.wait_ge(s_emb_t, g + 1)
                if g == 0:
                    pe.wait_ge(s_gram, 2)
                if g:
                    pe.wait_ge(s_prod, g)
                for n, _ in enumerate(new_gathers(g % BLOCKS)):
                    last = pe.matmul(gram_ps[:, n * P:(n + 1) * P], emb_t[:, g % 2, n * P:(n + 1) * P], gram[:],
                                     start=True, stop=True)
                last.then_inc(s_gram_rows, 1)

            def spread_rows(g):
                t, j = divmod(g, BLOCKS)
                pe.wait_ge(s_emb_n, g + 1)
                if g == 0:
                    pe.wait_ge(s_spread, len(SPREADS))
                if g:
                    pe.wait_ge(s_spr, HALVES * g)
                mine = [k for k, s in enumerate(SPREADS) if s[0] == j]
                for k in mine:
                    _, i, lo, n = SPREADS[k]
                    last = pe.matmul(spread_ps[:, lo * PROJ:(lo + n) * PROJ], emb_n[:, t % 2, i, :],
                                     spread[:, SPREAD_AT[k]:SPREAD_AT[k + 1], :], start=(k == mine[0]),
                                     stop=(k == mine[-1]), skip_group_check=True)
                last.then_inc(s_spread_ps, 1)

            def project(g, h):
                if g == 0 and h == 0:
                    pe.wait_ge(s_hd, H1 // P)
                    pe.wait_ge(s_proj_bs, HALVES)
                    pe.wait_ge(s_shift, HALVES)
                    pe.wait_ge(s_x_n, TILES)
                n = HALVES * g + h
                pe.wait_ge(s_spr, n + 1)
                if n >= 3:
                    pe.wait_ge(s_terms, n - 2)
                pe.matmul(proj_ps[n % 3][:], proj_high[:], spr[:, g % 2, h, 0, :], start=True, stop=False)
                pe.matmul(proj_ps[n % 3][:], proj_low[:, h, :], spr[:, g % 2, h, 1, :], start=False, stop=True)\
                  .then_inc(s_proj, 1)

            def pair(g):
                pe.wait_ge(s_terms, HALVES * (g + 1))
                if g == 0:
                    pe.wait_ge(s_xs, 1)
                if g:
                    pe.wait_ge(s_pairs, g)
                for n in range(MB):
                    b, q = divmod(n, 4)
                    m = q * (MB // 4) + b
                    last = pe.matmul(pair_ps[PROJ * q:PROJ * (q + 1), b * ZC:(b + 1) * ZC],
                                     terms[:, g % 2, m, 2:SLOTS], terms[:, g % 2, m, 0:ZC], start=True, stop=True,
                                     tile_position=(0, PROJ * q))
                last.then_inc(s_pair_ps, 1)

            def turn_feats(t, part):
                if part == 0:
                    pe.wait_ge(s_feats, 2 * t + 1)
                else:
                    pe.wait_ge(s_packed, t + 1)
                pe.wait_ge(*reader["turn_ps"])
                reader["turn_ps"] = (s_ft, 2 * t + part + 1)
                parts = ([feats[:, PROJ + n * P:PROJ + (n + 1) * P] for n in range(2)], [packed[:, n, :] for n in range(3)])
                for n, chunk in enumerate(parts[part]):
                    last = pe.transpose(turn_ps[:, n * P:(n + 1) * P], chunk, ident)
                last.then_inc(s_ft_ps, 1)

            def wide(t, part):
                if part < 2:
                    pe.wait_ge(s_ft, 2 * t + part + 1)
                if part == 0:
                    if t == 0:
                        pe.wait_ge(s_wl_g, CHUNKS)
                        pe.wait_ge(s_wl_aux, 3)
                    pe.wait_ge(*reader["wide_ps"])
                    reader["wide_ps"] = (s_z_n, t + 1)
                for k in ((0, 1), (2, 3), (4,))[part]:
                    last = pe.matmul(wide_ps[:], feats_t[:, k, :], wl[:, k, :], start=(k == 0), stop=(k == CHUNKS - 1))
                if part == 2:
                    last.then_inc(s_wide, 1)
                if part == 2 and t == TILES - 1:
                    pe.wait_ge(s_prod, BLOCKS_ALL)
                    for _ in range(CLOCK_PRODUCTS):
                        pe.matmul(gram_ps[:], ident, wl[:, 0, :], start=True, stop=True)

            def turn_z(t):
                pe.wait_ge(s_z_n, t + 1)
                pe.wait_ge(*reader["turn_ps"])
                reader["turn_ps"] = (s_z_t, ZK * (t + 1))
                for k in range(ZK):
                    last = pe.transpose(turn_ps[:, k * P:(k + 1) * P], z_n[:, k * P:(k + 1) * P], ident)
                last.then_inc(s_zt_ps, 1)

            def layer1(t):
                if t == 0:
                    pe.wait_ge(s_w12, 32)
                pe.wait_ge(*reader["wide_ps"])
                reader["wide_ps"] = (s_h1_sum, 2 * (t + 1))
                for k in range(ZK):
                    pe.wait_ge(s_z_t, ZK * t + k + 1)
                    for m in range(H1 // P):
                        last = pe.matmul(wide_ps[:, m * P:(m + 1) * P], w1[:, k, m * P:(m + 1) * P], z_t[:, k, :],
                                         start=(k == 0 and m == 0), stop=(k == ZK - 1), skip_group_check=True)
                last.then_inc(s_h1_ps, 1)

            def layer2(t):
                pe.wait_ge(*reader["wide_ps"])
                reader["wide_ps"] = (s_h2, t + 1)
                for k in range(H1 // P):
                    pe.wait_ge(s_h1, 2 * t + k // 2 + 1)
                    for m in range(H2 // P):
                        last = pe.matmul(wide_ps[:, m * P:(m + 1) * P], w2[:, k, m * P:(m + 1) * P], h1_t[:, k, :],
                                         start=(k == 0 and m == 0), stop=(k == H1 // P - 1), skip_group_check=True)
                last.then_inc(s_h2_ps, 1)

            def layer3(t):
                pe.wait_ge(s_h2, t + 1)
                pe.wait_ge(*reader["wide_ps"])
                reader["wide_ps"] = (s_y, t + 1)
                for k in range(H2 // P):
                    last = pe.matmul(wide_ps[0:1, 2 * P:3 * P], v("w3", k), h2_t[:, k, :],
                                     start=(k == 0), stop=(k == H2 // P - 1))
                last.then_inc(s_y_ps, 1)

            dense_layer1(0)
            turn(0)
            dense_layer1(1)
            for t in range(TILES):
                pe.wait_ge(s_x_n, t + 1)
                last = pe.transpose(wide_ps[:, t * P:(t + 1) * P], x_n[:, t, :], ident)
            last.then_inc(s_xt_ps, 1)
            for s in STEPS:
                for t in tiles(s - 10):
                    turn_z(t)
                for t in tiles(s - 8):
                    turn_feats(t, 0)
                for t in tiles(s - 12):
                    layer3(t)
                for t in tiles(s - 9):
                    turn_feats(t, 1)
                for g in blocks(s - 2):
                    spread_rows(g)
                for t in tiles(s - 8):
                    wide(t, 0)
                for t in tiles(s - 9):
                    wide(t, 1)
                for g in blocks(s - 3):
                    project(g, 1)
                for t in tiles(s - 9):
                    wide(t, 2)
                for t in tiles(s - 10):
                    layer1(t)
                if s == 2:
                    aux_weights()
                for g in blocks(s):
                    if g:
                        turn(g)
                for g in blocks(s - 4):
                    pair(g)
                if s == 0:
                    dense_layer1(2)
                for t in tiles(s - 11):
                    layer2(t)
                for g in blocks(s - 2):
                    project(g, 0)
                for g in blocks(s):
                    gram_rows(g)
                if s == 0:
                    sum_x()
                    dense_layer1(3)

        @block.scalar
        def _(act):
            act.wait_ge(s_zeroed, 6)
            act.activation(x_std[:, 0:1], eps[:], ACT.Sqrt).then_inc(s_warm, 1)
            act.wait_ge(s_ws_ps, 1)
            act.copy(ws_c[:], gram_ps[:, 0:P]).then_inc(s_ws_c, 1)
            act.wait_ge(s_gram_ps, 1)
            act.wait_ge(s_zeroed_w, 1)
            for h in range(HALVES):
                a = slice(h * D, (h + 1) * D)
                act.mul(gram[a, a], spread_ps[a, a], 1.0 / E).then_inc(s_gram, 1)
            act.wait_ge(s_proj_ps, 1)
            act.copy(proj_high[:], proj_ps[0][:, 0:E]).then_inc(s_proj_w, 1)
            act.wait_ge(s_shift_ps, 1)
            act.copy(sum_high[:], pair_ps[:, 0:PROJ]).then_inc(s_sum_high, 1)
            act.wait_ge(s_vec, 16)
            for n in range(TILES // 2):
                act.wait_ge(s_dt_ps, n + 1)
                act.copy(dense_t[:, 2 * n:2 * n + 2, :, :],
                         proj_ps[1 + n][:].rearrange("p (t k b) -> p t k b", t=2, k=DK)).then_inc(s_dt, 1)
            act.wait_ge(s_x_mv, TILES)
            act.wait_ge(s_warm, 1)
            act.activation(x_std[:], x_mv[:, :, 1], ACT.Sqrt, bias=eps[:]).then_inc(s_x_std, 1)
            def copy_dense_layer1(m):
                act.wait_ge(s_hd_ps, m + 1)
                act.activation(h1_dense[:, m, :], proj_ps[1 + m % 2][:], ACT.Identity, bias=v("b1", m)).then_inc(s_hd, 1)

            def copy_shift():
                act.wait_ge(s_sum_parts, 1)
                for h in range(HALVES):
                    b = slice((1 - h) * D, (2 - h) * D)
                    for parity in range(2):
                        last = act.copy(spr[b, parity, h, 1, :].rearrange("o (b p) -> o b p", p=PROJ),
                                        sum_parts[b, :].unsqueeze(1).to_broadcast([D, BS, PROJ]))
                    last.then_inc(s_shift, 1)

            def copy_sums():
                act.wait_ge(s_xs_ps, 1)
                act.copy(x_sum[:], pair_ps[:, 0:TILES]).then_inc(s_xs, 1)

            def copy_turned(g):
                act.wait_ge(s_turn, g + 1)
                if g >= 2:
                    act.wait_ge(s_gram_rows, g - 1)
                n = len(new_gathers(g % BLOCKS)) * P
                act.copy(emb_t[:, g % 2, 0:n], turn_ps[:, 0:n]).then_inc(s_emb_t, 1)

            def copy_spread(g):
                act.wait_ge(s_spread_ps, g + 1)
                if g >= 2:
                    act.wait_ge(s_proj, HALVES * (g - 1))
                for h in range(HALVES):
                    a = slice(h * D, (h + 1) * D)
                    act.copy(spr[a, g % 2, h, :, :], spread_ps[a, :].unsqueeze(1).to_broadcast([D, 2, COLS]))\
                       .then_inc(s_spr_high, 1)

            def row_std(g):
                act.wait_ge(s_var_e, g + 1)
                n = HALVES * len(new_gathers(g % BLOCKS))
                act.activation(var_c[:, 0:n], var_e[:, 0:n], ACT.Relu).then_inc(s_var_c, 1)
                act.wait_ge(s_var_c, g + 1)
                if g:
                    act.wait_ge(s_rstd_e, g)
                act.activation(std_e[:, 0:n], var_c[:, 0:n], ACT.Sqrt, bias=eps[:]).then_inc(s_std_e, 1)

            def proj_std(g):
                act.wait_ge(s_var_p, HALVES * (g + 1))
                if g:
                    act.wait_ge(s_rstd_p, g)
                act.activation(std_p[:], var_p[:], ACT.Sqrt, bias=eps[:], scale=1.0 / PROJ).then_inc(s_std_p, 1)

            def z_std(t):
                act.wait_ge(s_z_mv, t + 1)
                act.activation(z_std_sb[:], z_mv[:, 1:2], ACT.Sqrt, bias=eps[:]).then_inc(s_z_std, 1)

            def normalise_z(t):
                act.wait_ge(s_z_shift, t + 1)
                if t:
                    act.wait_ge(s_zt_ps, t)
                act.activation(z_n[:], wide_ps[:, 0:DIMS], ACT.Identity, bias=z_shift[:], scale=z_rstd[:])\
                   .then_inc(s_z_n, 1)

            def squares(g, h):
                n = HALVES * g + h
                if g:
                    act.wait_ge(s_var_p, n - 1)
                act.wait_ge(s_proj, n + 1)
                act.activation(sq[:, h * BS:(h + 1) * BS, :],
                               proj_ps[n % 3][:].rearrange("e (b p) -> e b p", p=PROJ), ACT.Square).then_inc(s_sq, 1)

            def copy_pairs(g):
                t, j = divmod(g, BLOCKS)
                act.wait_ge(s_pair_ps, g + 1)
                if j == 0 and t:
                    act.wait_ge(s_feats, 2 * t)
                n = MB // 4
                act.copy(pairs[:, :, j * n:(j + 1) * n].rearrange("p j b -> p b j"),
                         pair_ps[:, 0:n * ZC].rearrange("p (b j) -> p b j", j=ZC)).then_inc(s_pairs, 1)

            def pack_pairs(t):
                act.wait_ge(s_feats, 2 * (t + 1))
                if t:
                    act.wait_ge(s_ft_ps, 2 * t)
                grid = feats[:, PROJ:].rearrange("b (j i) -> b j i", i=PROJ)
                for n, at, j0, j1, i0, i1 in ((0, 0, 8, 12, 8, 24), (0, 64, 12, 16, 12, 24), (1, 0, 20, 24, 20, 32),
                                              (1, 64, 16, 20, 16, 32), (2, 0, 8, 16, 24, 32), (2, 80, 24, 28, 24, 32),
                                              (2, 112, 28, 32, 28, 32)):
                    run = packed[:, n, at:at + (j1 - j0) * (i1 - i0)]
                    act.copy(run.rearrange("b (j i) -> b j i", i=i1 - i0), grid[:, j0:j1, i0:i1])
                act.copy(packed[:, 2, SX_AT[1]:SX_AT[1] + 1], x_sum[:, t:t + 1])
                for chunk, at, i in SUM_AT:
                    last = act.copy(packed[:, chunk - 2, at:at + 16], feats[:, i:i + 16])
                last.then_inc(s_packed, 1)

            def copy_feats(t, part):
                act.wait_ge(s_ft_ps, 2 * t + part + 1)
                if part == 0 and t:
                    act.wait_ge(s_wide, t)
                a, b = ((0, 2), (2, CHUNKS))[part]
                act.copy(feats_t[:, a:b, :], turn_ps[:, 0:(b - a) * P].rearrange("p (k b) -> p k b", b=P))\
                   .then_inc(s_ft, 1)

            def scale_z(t):
                act.wait_ge(s_zt_ps, t + 1)
                if t:
                    act.wait_ge(s_h1_ps, t)
                for k in range(ZK):
                    act.activation(z_t[:, k, :], turn_ps[:, k * P:(k + 1) * P], ACT.Identity,
                                   bias=v("bl", k), scale=v("gl", k)).then_inc(s_z_t, 1)

            def relu1(t):
                if t:
                    act.wait_ge(s_h2_ps, t)
                for n in range(2):
                    act.wait_ge(s_h1_sum, 2 * t + n + 1)
                    act.activation(h1_t[:, 2 * n:2 * n + 2, :], h1_sum[:, 2 * n:2 * n + 2, :], ACT.Relu).then_inc(s_h1, 1)

            def relu2(t):
                act.wait_ge(s_h2_ps, t + 1)
                if t:
                    act.wait_ge(s_y_ps, t)
                for m in range(H2 // P):
                    last = act.activation(h2_t[:, m, :], wide_ps[:, m * P:(m + 1) * P], ACT.Relu, bias=v("b2", m))
                last.then_inc(s_h2, 1)

            def copy_y(t):
                act.wait_ge(s_y_ps, t + 1)
                src = wide_ps[0:1, 2 * P:3 * P].rearrange("o (h q j b) -> o h j q b", h=2, q=2, j=BLOCKS)
                dst = y_row[0:1, t * P:(t + 1) * P].rearrange("o (h j q b) -> o h j q b", h=2, q=2, j=BLOCKS)
                for h in range(2):
                    last = act.copy(dst[:, h], src[:, h])
                last.then_inc(s_y, 1)

            copy_dense_layer1(0)
            copy_turned(0)
            copy_dense_layer1(1)
            act.wait_ge(s_xt_ps, 1)
            act.activation(x_t[:], wide_ps[:].rearrange("e (t b) -> e t b", b=P), ACT.Identity, bias=v("bd"),
                           scale=v("gd")).then_inc(s_xt, 1)
            for s in STEPS:
                for t in tiles(s - 7):
                    copy_feats(t, 0)
                for t in tiles(s - 11):
                    copy_y(t)
                for t in tiles(s - 10):
                    relu1(t)
                for t in tiles(s - 7):
                    pack_pairs(t)
                if s == 0:
                    copy_sums()
                    copy_dense_layer1(3)
                for t in tiles(s - 9):
                    scale_z(t)
                for g in blocks(s - 1):
                    copy_spread(g)
                for g in blocks(s - 2):
                    squares(g, 1)
                for g in blocks(s):
                    row_std(g)
                for t in tiles(s - 8):
                    z_std(t)
                for g in blocks(s + 1):
                    if g:
                        copy_turned(g)
                for g in blocks(s - 2):
                    proj_std(g)
                for t in tiles(s - 8):
                    normalise_z(t)
                for g in blocks(s - 3):
                    copy_pairs(g)
                for t in tiles(s - 7):
                    copy_feats(t, 1)
                if s == 0:
                    copy_dense_layer1(2)
                    copy_shift()
                for t in tiles(s - 10):
                    relu2(t)
                for g in blocks(s - 1):
                    squares(g, 0)

        @block.vector
        def _(dve):
            dve.wait_ge(s_ids, 32)
            dve.tensor_tensor(idx[:], ids_raw[:], ids_off[:], ALU.add).then_inc(s_idx, 1)
            dve.memset(gram[:], 0.0).then_inc(s_zeroed_w, 1)
            dve.wait_ge(s_vec, 16)
            dve.wait_ge(s_ws_c, 1)
            dve.tensor_scalar(ws_cg[:], ws_c[:], v("gs"), None, ALU.mult).then_inc(s_ws_cg, 1)
            dve.wait_ge(s_wsi, 16)
            dve.tensor_reduce(wsi_mean[:], wsi_raw[:], AX.X, ALU.add).then_inc(s_wsi_mean, 1)
            dve.wait_ge(s_wsi_mean, 1)
            dve.tensor_scalar(wsi_m[:], wsi_mean[:], 1.0 / PROJ, None, ALU.mult).then_inc(s_wsi_m, 1)
            dve.wait_ge(s_wsi_m, 1)
            dve.tensor_tensor(wsi_c[:], wsi_raw[:], wsi_m[:].unsqueeze(2).to_broadcast([P, GATHERS, PROJ]),
                              ALU.subtract).then_inc(s_wsi_c, 1)
            dve.wait_ge(s_proj_w, 1)
            for h in range(HALVES):
                a = slice(h * D, (h + 1) * D)
                dve.tensor_tensor(proj_low[a, h, :], proj_ps[0][a, 0:E], proj_high[a, :].bitcast(F32), ALU.subtract)\
                   .then_inc(s_proj_low, 1)
            dve.wait_ge(s_con, 16)
            def pair_weights():
                a, b = VEC["gj"]
                dve.tensor_tensor(gj0[:], vec[:, a:b], c("not_x"), ALU.mult).then_inc(s_pair_v, 1)
                a, b = VEC["bj"]
                dve.tensor_tensor(bj[:], vec[:, a:b], c("not_x"), ALU.mult).then_inc(s_pair_v, 1)
                dve.wait_ge(s_pair_v, 2)
                dve.tensor_tensor(gj[:], gj0[:], c("is_x"), ALU.add).then_inc(s_pair_v, 1)
                dve.wait_ge(s_pair_v, 3)
                a, b = VEC["gi"]
                dve.tensor_tensor(gij[:], vec[:, a:b], gj[:], ALU.mult).then_inc(s_pair_v, 1)
                dve.wait_ge(s_zeroed, 6)
                for k in range(CHUNKS):
                    pick_i = c("pick_i")[:, k * PROJ:(k + 1) * PROJ]
                    pick_j = c("pick_j")[:, k * PROJ:(k + 1) * PROJ]
                    dve.tensor_scalar(aux_i[:, k, :], pick_i, v("gi", k), bj[:, k:k + 1], ALU.mult, ALU.mult)
                    dve.tensor_scalar(aux_j[:, k, :], pick_j, v("bi", k), gj[:, k:k + 1], ALU.mult, ALU.mult)\
                       .then_inc(s_aux_ij, 1)
                dve.wait_ge(s_aux_ij, CHUNKS)
                a, b = VEC["bi"]
                for _, at, i in SUM_AT:
                    dve.tensor_tensor(aux_w[:, :, at:at + 16], aux_i[:, :, i:i + 16], aux_j[:, :, i:i + 16], ALU.add)\
                       .then_inc(s_aux_w, 1)
                dve.tensor_tensor(aux_w[:, :, SX_AT[1]], vec[:, a:b], c("is_x"), ALU.mult).then_inc(s_aux_w, 1)
                dve.scalar_tensor_tensor(aux_w[:, :, ONE_AT[1]], vec[:, a:b], float(E), bj[:], ALU.mult, ALU.mult)\
                   .then_inc(s_aux_w, 1)
            pair_weights()
            dve.wait_ge(s_sum_high, 1)
            dve.tensor_tensor(sum_low[:], pair_ps[:, 0:PROJ], sum_high[:].bitcast(F32), ALU.subtract)\
               .then_inc(s_sum_low, 1)
            dve.wait_ge(s_x_ps, 1)
            for t in range(TILES):
                dve.bn_stats(x_stats[:, t, :], proj_ps[0][:, t * P:(t + 1) * P]).then_inc(s_x_stats, 1)
            for t in range(TILES):
                dve.wait_ge(s_x_stats, t + 1)
                dve.bn_aggr(x_mv[:, t, :], x_stats[:, t, :]).then_inc(s_x_mv, 1)
            dve.wait_ge(s_x_std, 1)
            dve.reciprocal(x_rstd[:], x_std[:]).then_inc(s_x_rstd, 1)
            dve.wait_ge(s_x_rstd, 1)
            for t in range(TILES):
                dve.tensor_scalar(x_n[:, t, :], proj_ps[0][:, t * P:(t + 1) * P], x_mv[:, t, 0:1], x_rstd[:, t:t + 1],
                                  ALU.subtract, ALU.mult).then_inc(s_x_n, 1)

            dve.wait_ge(s_wsi_c, 1)
            for k, (_, i, _, n) in enumerate(SPREADS):
                mask = c("spread")[:, SPREAD_AT[k]:SPREAD_AT[k + 1]]
                dve.tensor_tensor(spread[:, SPREAD_AT[k]:SPREAD_AT[k + 1], :],
                                  mask.unsqueeze(2).to_broadcast([P, n, PROJ]),
                                  wsi_c[:, i:i + 1, :].to_broadcast([P, n, PROJ]), ALU.mult).then_inc(s_spread, 1)


            def bias_parts():
                dve.tensor_scalar(sum_part[:], sum_high[:].bitcast(F32), c("high_v"), None, ALU.mult).then_inc(s_sum_part, 1)
                dve.wait_ge(s_sum_low, 1)
                dve.wait_ge(s_sum_part, 1)
                dve.scalar_tensor_tensor(sum_parts[:], sum_low[:], c("low_v"), sum_part[:], ALU.mult, ALU.add)\
                   .then_inc(s_sum_parts, 1)
                dve.wait_ge(s_bs, 16)
                dve.tensor_copy(bs_high[:], bs_sb[:]).then_inc(s_bs_high, 1)
                dve.wait_ge(s_bs_high, 1)
                dve.tensor_tensor(bs_low[:], bs_sb[:], bs_high[:].bitcast(F32), ALU.subtract).then_inc(s_bs_low, 1)
                dve.tensor_scalar(bs_part[:], bs_high[:].bitcast(F32), c("high_w"), None, ALU.mult).then_inc(s_bs_part, 1)
                dve.wait_ge(s_bs_low, 1)
                dve.wait_ge(s_bs_part, 1)
                for h in range(HALVES):
                    b = slice((1 - h) * D, (2 - h) * D)
                    dve.scalar_tensor_tensor(proj_low[b, h, :], bs_low[b, :], c("low_w")[b, :], bs_part[b, :], ALU.mult,
                                             ALU.add).then_inc(s_proj_bs, 1)

            def scale_wl():
                dve.wait_ge(s_pair_v, 4)
                dve.wait_ge(s_wl_aux_ps, 1)
                for k in reversed(range(CHUNKS)):
                    dve.tensor_scalar(wl[:, k, :], wl[:, k, :], gij[:, k:k + 1], None, ALU.mult).then_inc(s_wl_g, 1)
                for n, k in enumerate((4, 3, 2)):
                    dve.wait_ge(s_wl_g, n + 1)
                    dve.scalar_tensor_tensor(wl[:, k, :], wide_ps[:], c("sum_rows")[:, k:k + 1], wl[:, k, :], ALU.mult,
                                             ALU.add).then_inc(s_wl_aux, 1)

            def row_products(g):
                t, j = divmod(g, BLOCKS)
                rows = new_gathers(j)
                w = len(rows)
                dve.wait_ge(s_gram_rows, g + 1)
                if g:
                    dve.wait_ge(s_var_e, g)
                dve.tensor_tensor(prod[:, 0:w * P].rearrange("p (i c) -> p i c", c=P),
                                  gram_ps[:, 0:w * P].rearrange("p (i c) -> p i c", c=P),
                                  emb[:, t, rows[0]:rows[0] + w, :], ALU.mult).then_inc(s_prod, 1)

            def row_variances(g):
                w = len(new_gathers(g % BLOCKS))
                dve.wait_ge(s_prod, g + 1)
                if g:
                    dve.wait_ge(s_var_c, g)
                dve.tensor_reduce(var_e[:, 0:2 * w], prod[:, 0:w * P].rearrange("p (n d) -> p n d", d=D), AX.X,
                                  ALU.add).then_inc(s_var_e, 1)

            def normalise_rows(g):
                t, j = divmod(g, BLOCKS)
                rows = new_gathers(j)
                w = len(rows)
                e = emb[:, t, rows[0]:rows[0] + w, :]
                dve.wait_ge(s_std_e, g + 1)
                dve.reciprocal(rstd_e[:, 0:2 * w], std_e[:, 0:2 * w]).then_inc(s_rstd_e, 1)
                dve.wait_ge(s_rstd_e, g + 1)
                if t >= 2:
                    dve.wait_ge(s_spread_ps, (t - 1) * BLOCKS)
                dve.tensor_tensor(emb_n[:, t % 2, rows[0]:rows[0] + w, :].rearrange("p i (h d) -> p (i h) d", d=D),
                                  e.rearrange("p i (h d) -> p (i h) d", d=D),
                                  rstd_e[:, 0:2 * w].unsqueeze(2).to_broadcast([P, 2 * w, D]), ALU.mult)\
                   .then_inc(s_emb_n, 1)

            def low_spread(g):
                for h in range(HALVES):
                    a, b = slice(h * D, (h + 1) * D), slice((1 - h) * D, (2 - h) * D)
                    dve.wait_ge(s_spr_high, HALVES * g + h + 1)
                    dve.tensor_tensor(spr[b, g % 2, h, 0, :], spread_ps[a, :], spr[a, g % 2, h, 0, :].bitcast(F32),
                                      ALU.subtract).then_inc(s_spr, 1)

            def proj_variances(g, h):
                dve.wait_ge(s_sq, HALVES * g + h + 1)
                if g:
                    dve.wait_ge(s_std_p, g)
                a = slice(h * BS, (h + 1) * BS)
                dve.tensor_reduce(var_p[:, a], sq[:, a, :], AX.X, ALU.add).then_inc(s_var_p, 1)

            def proj_rstd(g):
                t, j = divmod(g, BLOCKS)
                if g >= 2:
                    dve.wait_ge(s_pair_ps, g - 1)
                if g == 0:
                    dve.wait_ge(s_xt, 1)
                x = x_t[:, t, :].rearrange("e (q j b) -> e q j b", q=4, j=BLOCKS)[:, :, j, :]
                dve.tensor_copy(terms[:, g % 2, :, 1].rearrange("e (q b) -> e q b", q=4), x)
                dve.wait_ge(s_std_p, g + 1)
                if g:
                    dve.wait_ge(s_terms, HALVES * g)
                dve.reciprocal(rstd_p[:], std_p[:]).then_inc(s_rstd_p, 1)

            def normalise_proj(g, h):
                dve.wait_ge(s_rstd_p, g + 1)
                a = slice(h * BS, (h + 1) * BS)
                dve.tensor_tensor(terms[:, g % 2, a, 2:SLOTS],
                                  proj_ps[(HALVES * g + h) % 3][:].rearrange("e (b p) -> e b p", p=PROJ),
                                  rstd_p[:, a].unsqueeze(2).to_broadcast([E, BS, PROJ]), ALU.mult)\
                   .then_inc(s_terms, 1)

            def turn_pairs(t, part):
                if part == 0:
                    dve.wait_ge(s_pairs, BLOCKS * (t + 1))
                    if t:
                        dve.wait_ge(s_ft_ps, 2 * t)
                a, b = ((0, 9), (9, ZC))[part]
                dve.transpose(feats[:, a * PROJ:b * PROJ], pairs[:, a:b, :].rearrange("p j b -> p (j b)"))\
                   .then_inc(s_feats, 1)

            def z_variances(t):
                dve.wait_ge(s_wide, t + 1)
                dve.bn_stats(z_stats[:], wide_ps[:]).then_inc(s_z_stats, 1)
                dve.wait_ge(s_z_stats, t + 1)
                dve.bn_aggr(z_mv[:], z_stats[:]).then_inc(s_z_mv, 1)

            def z_scales(t):
                dve.wait_ge(s_z_std, t + 1)
                if t:
                    dve.wait_ge(s_z_n, t)
                dve.reciprocal(z_rstd[:], z_std_sb[:]).then_inc(s_z_rstd, 1)
                dve.wait_ge(s_z_rstd, t + 1)
                dve.scalar_tensor_tensor(z_shift[:], z_mv[:, 0:1], -1.0, z_rstd[:], ALU.mult, ALU.mult)\
                   .then_inc(s_z_shift, 1)

            def add_dense(t):
                dve.wait_ge(s_h1_ps, t + 1)
                if t == 0:
                    dve.wait_ge(s_hd, H1 // P)
                if t:
                    dve.wait_ge(s_h1, 2 * t)
                for n in range(2):
                    dve.tensor_tensor(h1_sum[:, 2 * n:2 * n + 2, :],
                                      wide_ps[:, 2 * n * P:2 * (n + 1) * P].rearrange("p (m b) -> p m b", b=P),
                                      h1_dense[:, 2 * n:2 * n + 2, t * P:(t + 1) * P], ALU.add).then_inc(s_h1_sum, 1)

            for s in STEPS:
                for g in blocks(s - 5):
                    normalise_proj(g, 1)
                for g in blocks(s - 4):
                    proj_variances(g, 0)
                for g in blocks(s - 2):
                    row_variances(g)
                if s == 2:
                    bias_parts()
                for g in blocks(s - 3):
                    low_spread(g)
                for t in tiles(s - 10):
                    z_variances(t)
                for g in blocks(s - 4):
                    proj_variances(g, 1)
                for t in tiles(s - 10):
                    z_scales(t)
                for g in blocks(s - 2):
                    normalise_rows(g)
                for t in tiles(s - 8):
                    turn_pairs(t, 0)
                for g in blocks(s - 4):
                    proj_rstd(g)
                for t in tiles(s - 8):
                    turn_pairs(t, 1)
                for g in blocks(s - 4):
                    normalise_proj(g, 0)
                if s == 3:
                    scale_wl()
                for t in tiles(s - 11):
                    add_dense(t)
                for g in blocks(s - 1):
                    row_products(g)


def layout(inputs):
    tables = [np.asarray(inputs[f"tbl_{k}"]) for k in range(NT)]
    get = {k: np.asarray(a) for k, a in inputs.items() if not k.startswith("tbl_")}
    a = {"table": np.concatenate(tables, axis=0)}
    first = np.concatenate([[0], np.cumsum([x.shape[0] for x in tables])])[:NT]
    n = TILES * HALVES * GATHERS
    a["ids"] = get["ids"].reshape(n, P).T
    a["offsets"] = np.tile(first, BATCH).reshape(n, P).T.astype(np.int32)
    a["dense"] = get["r_dense_t"].reshape(TILES, 2, BLOCKS, 2, 8, DENSE).transpose(0, 1, 3, 2, 4, 5)\
        .reshape(TILES, P, DENSE)
    a["wd_t"] = get["L0_rec_Wd"].T
    a["ws2"] = np.concatenate([get["L0_rec_Ws"]] * 2, axis=1)
    a["wsi_rep"] = np.tile(get["L0_rec_Wsi"].T, (HALF, 1)).reshape(GATHERS, P, PROJ)
    a["bs_rep"] = np.tile(get["L0_rec_bs"].reshape(1, E), (P, 1))
    chunks = pair_chunks()
    wl_t = get["L0_rec_Wl"].T
    packed = np.zeros((CHUNKS, P, MAXD), np.float32)
    con = np.zeros((P, CONS), np.float32)
    vec = np.zeros((P, VECS), np.float32)

    def cols(name, k=0, w=1):
        return slice(CON[name][0] + k * w, CON[name][0] + (k + 1) * w)

    for k, chunk in enumerate(chunks):
        pair = np.array([x is not None for x in chunk])
        j, i = np.array([x or (0, 0) for x in chunk]).T
        live = pair & (i >= j)
        packed[k, live] = wl_t[(i * (i + 1) // 2 + j)[live]]
        con[np.arange(P), CON["pick_i"][0] + k * PROJ + i] = pair
        y = pair & (j >= 1)
        con[np.arange(P)[y], CON["pick_j"][0] + k * PROJ + j[y] - 1] = 1.0
        con[:, CON["is_x"][0] + k] = pair & (j == 0)
        con[:, CON["not_x"][0] + k] = y
        for name, src, at in (("gi", "gsi", i), ("bi", "bsi", i), ("gj", "gsi", np.maximum(j - 1, 0)),
                              ("bj", "bsi", np.maximum(j - 1, 0))):
            vec[:, VEC[name][0] + k] = get[f"L0_rec_{src}"][at]
    for chunk, at, _ in SUM_AT + ((*SX_AT, 1), (*ONE_AT, 1)):
        con[at:at + (16 if chunk < 4 else 1), CON["sum_rows"][0] + chunk] = 1.0
    a["wl_t"] = packed.reshape(CHUNKS * P, MAXD)
    con[:, CON["ident"][0]:CON["ident"][1]] = np.eye(P)
    con[:, CON["centre"][0]:CON["centre"][1]] = np.eye(P) - 1.0 / P
    for name, rows in (("high_w", (0, 1)), ("low_w", (2,)), ("high_v", (0, 2)), ("low_v", (1,))):
        for row in rows:
            con[row::D, CON[name][0]] = 1.0
    for k, (j, i, lo, m) in enumerate(SPREADS):
        sample = (i * P + np.arange(P)) // NT - j * BS - lo
        ok = (sample >= 0) & (sample < m)
        con[np.arange(P)[ok], CON["spread"][0] + SPREAD_AT[k] + sample[ok]] = 1.0
    for name, src, w in (("gs", "L0_rec_gs", 1), ("gd", "L0_rec_gd", 1), ("bd", "L0_rec_bd", 1),
                         ("gl", "L0_rec_gl", ZK), ("bl", "L0_rec_bl", ZK), ("b1", "b_top1", H1 // P),
                         ("b2", "b_top2", H2 // P), ("w3", "W_top3", H2 // P)):
        vec[:, VEC[name][0]:VEC[name][1]] = get[src].reshape(-1, P)[:w].T
    a["consts"], a["vecs"] = con, vec
    w_top1 = get["W_top1"]
    a["w1_t"] = np.concatenate([w_top1[0:DIMS], w_top1[MAXD:]], axis=0)
    a["w2_t"] = get["W_top2"]
    return a


_INS = ["table", "ids", "offsets", "dense", "consts", "vecs", "bs_rep", "wd_t", "ws2", "wsi_rep", "wl_t", "w1_t", "w2_t"]


def kernel(**inputs):
    import concourse.bacc as bacc
    from concourse.bass_utils import run_bass_kernel_spmd

    nc = bacc.Bacc("TRN2", target_bir_lowering=False, num_devices=1)
    arrays, args = {}, []
    for name, a in layout(inputs).items():
        arrays[f"in_{name}"] = np.ascontiguousarray(a)
    for name in _INS:
        a = arrays[f"in_{name}"]
        args.append(nc.dram_tensor(f"in_{name}", a.shape, mybir.dt.from_np(a.dtype), kind="ExternalInput").ap())
    out = nc.dram_tensor("out_y", (1, BATCH), F32, kind="ExternalOutput").ap()
    build(nc, *args, out)
    r = run_bass_kernel_spmd(nc, [arrays], core_ids=[0])
    return r.results[0]["out_y"].reshape(BATCH, 1)
```
